# Optimizing a Trainium2 kernel written in Bass

```python
import numpy as np
import jax
import jax.numpy as jnp

def _softmax(x, axis=-1):
    return jax.nn.softmax(x, axis=axis)

def _gelu(x):
    return jax.nn.gelu(x, approximate=True)

def _silu(x):
    return jax.nn.silu(x)

def _sigmoid(x):
    return jax.nn.sigmoid(x)

def _layernorm(x, axis=-1, eps=1e-05):
    m = jnp.mean(x, axis=axis, keepdims=True)
    v = jnp.var(x, axis=axis, keepdims=True)
    return (x - m) / jnp.sqrt(v + eps)

def _scatter_add(tgt, idx, src, axis=0):
    return tgt.at[idx].add(src)

def _segment_sum(src, seg, n):
    return jax.ops.segment_sum(src, seg, n)
kernel_name = 'mk_seq_postln_d1_jaxref_r8_20f42c'

def setup_inputs(seed: int=0):
    np.random.seed(seed)
    _w = jnp.asarray

    def _L0_attn_setup():
        import jax, jax.numpy as jnp
        import numpy as np
        import math
        B, T, E = (1, 256, 128)
        H = 16
        D = E // H
        L = 64
        key = jax.random.key(seed)
        ks = jax.random.split(key, 7)
        s = lambda fan: 1.0 / math.sqrt(fan)
        return {'hidden_states': jax.random.normal(ks[0], (B, T, E), dtype=jnp.float32), 'Wq': jax.random.normal(ks[1], (E, E), dtype=jnp.float32) * s(E), 'Wk_down': jax.random.normal(ks[2], (L, E), dtype=jnp.float32) * s(E), 'Wv_down': jax.random.normal(ks[3], (L, E), dtype=jnp.float32) * s(E), 'q_to_latent': jax.random.normal(ks[4], (H, D, L), dtype=jnp.float32) * s(D), 'v_up': jax.random.normal(ks[5], (H, L, D), dtype=jnp.float32) * s(L), 'Wout': jax.random.normal(ks[6], (E, E), dtype=jnp.float32) * s(E)}
    _L0_attn_in = _L0_attn_setup()

    def _L0_ffn_setup():
        import jax, jax.numpy as jnp
        import numpy as np
        FP8_MAX = 448.0
        SCALE = 1.0
        _FP8_DTYPE = getattr(jnp, 'float8_e4m3fn', jnp.float16)

        def quantize_e4m3(t, scale):
            return jnp.clip(t / scale, -FP8_MAX, FP8_MAX).astype(_FP8_DTYPE)
        key = jax.random.key(seed)
        kx, kw = jax.random.split(key)
        B, N, C, F = (8, 512, 128, 128)
        x = jax.random.normal(kx, (B, N, C), dtype=jnp.float32)
        weight = jax.random.normal(kw, (F, C), dtype=jnp.float32) * 0.02
        bias = jnp.zeros((F,), dtype=jnp.float32)
        return {'x': x, 'weight': weight, 'bias': bias}
    _L0_ffn_in = _L0_ffn_setup()
    _d = {'L0_attn_hidden_states': _L0_attn_in['hidden_states'], 'L0_attn_Wq': _L0_attn_in['Wq'], 'L0_attn_Wk_down': _L0_attn_in['Wk_down'], 'L0_attn_Wv_down': _L0_attn_in['Wv_down'], 'L0_attn_q_to_latent': _L0_attn_in['q_to_latent'], 'L0_attn_v_up': _L0_attn_in['v_up'], 'L0_attn_Wout': _L0_attn_in['Wout'], 'L0_ffn_weight': _L0_ffn_in['weight'], 'L0_ffn_bias': _L0_ffn_in['bias']}
    _x0 = _d['L0_attn_hidden_states']
    _d['L0_attn_hidden_states'] = jax.random.normal(jax.random.fold_in(jax.random.key(seed), 1), (1, 2048, 128), dtype=_x0.dtype)
    del _x0
    return _d

def reference(L0_attn_hidden_states, L0_attn_Wq, L0_attn_Wk_down, L0_attn_Wv_down, L0_attn_q_to_latent, L0_attn_v_up, L0_attn_Wout, L0_ffn_weight, L0_ffn_bias):

    def _L0_attn_ref(hidden_states, Wq, Wk_down, Wv_down, q_to_latent, v_up, Wout):
        import jax, jax.numpy as jnp
        import numpy as np
        import math
        B, T, E = (1, 256, 128)
        H = 16
        D = E // H
        L = 64
        'RA_MLA_Attention forward (default config: coupling_scale=0 so the RA\n            reciprocal-band branch is inactive; no cache, no RoPE, dropout=0).'
        b, t, e = hidden_states.shape
        h, d, l = q_to_latent.shape
        Q = (hidden_states @ Wq.T).reshape(b, t, h, d)
        latent_k = hidden_states @ Wk_down.T
        latent_v = hidden_states @ Wv_down.T
        q_lat = jnp.einsum('bthd,hdl->bthl', Q, q_to_latent)
        logits = jnp.einsum('bthl,bsl->bhts', q_lat, latent_k) / math.sqrt(l)
        causal = jnp.tril(jnp.ones((t, t), dtype=bool))
        logits = jnp.where(causal[None, None], logits, jnp.float32(-1e+30))
        attn = jax.nn.softmax(logits, axis=-1)
        ctx_lat = jnp.einsum('bhts,bsl->bhtl', attn, latent_v)
        heads = jnp.einsum('bhtl,hld->bthd', ctx_lat, v_up)
        out = heads.reshape(b, t, h * d) @ Wout.T
        return out

    def _L0_ffn_ref(x, weight, bias):
        import jax, jax.numpy as jnp
        import numpy as np
        FP8_MAX = 448.0
        SCALE = 1.0
        _FP8_DTYPE = getattr(jnp, 'float8_e4m3fn', jnp.float16)

        def quantize_e4m3(t, scale):
            return jnp.clip(t / scale, -FP8_MAX, FP8_MAX).astype(_FP8_DTYPE)
        B, N, C = x.shape
        x2d = x.reshape(B * N, C)
        x_mat = quantize_e4m3(x2d, SCALE).astype(jnp.float16)
        w_mat = quantize_e4m3(weight, SCALE).astype(jnp.float16)
        out2d = (x_mat @ w_mat.T).astype(jnp.float32) * (SCALE * SCALE)
        out2d = out2d + bias
        return out2d.reshape(B, N, -1)
    x = L0_attn_hidden_states
    x = _layernorm(x + _L0_attn_ref(x, L0_attn_Wq, L0_attn_Wk_down, L0_attn_Wv_down, L0_attn_q_to_latent, L0_attn_v_up, L0_attn_Wout), axis=-1)
    x = _layernorm(x + _L0_ffn_ref(x, L0_ffn_weight, L0_ffn_bias), axis=-1)
    return x

_drawn_inputs = setup_inputs


def setup_inputs(seed=0):
    import zlib

    import numpy as np

    out = dict(_drawn_inputs(seed))
    spreads = {'L0_ffn_bias': (0.0, 0.1)}
    factors = {}
    for name, (base, spread) in spreads.items():
        noise = np.random.default_rng([zlib.crc32(name.encode()), seed]).standard_normal(out[name].shape)
        drawn = base * np.exp(spread * noise) if base else spread * noise
        out[name] = jnp.asarray(drawn.astype(out[name].dtype))
    for name, factor in factors.items():
        out[name] = (out[name] * factor).astype(out[name].dtype)
    return out
```

```python
import concourse.bass as bass
from concourse import mybir
from contextlib import ExitStack


def postln_block_kernel(nc, x, xT, wqT, wk_down, wv_down, q2lT, v_upT, woutT, ffn_wT, ffn_bias, out):
    f32, bf16, f16 = mybir.dt.float32, mybir.dt.bfloat16, mybir.dt.float16
    fp8 = mybir.dt.float8e4
    ALU, ACT, AX = mybir.AluOpType, mybir.ActivationFunctionType, mybir.AxisListType

    T, E = x.shape
    L = wk_down.shape[0]
    H = 16
    D = E // H
    BT = 128
    NB = T // BT
    CW = 512
    NC = T // CW
    BC = CW // BT
    PARTS = 3
    ROWS = PARTS * PARTS * D
    AUG = ROWS + PARTS
    VW = 32
    SCALE = 1.0 / 8.0
    EPS = 1e-5
    assert L == 64 and ROWS == 72

    S_TILES = [(i, c, min(CW, (i + 1) * BT - c * CW)) for i in range(NB) for c in range(i // BC + 1)]
    NS = len(S_TILES)
    GROUPS = [(c, g) for c in range(NC) for g in range(c + 1)]
    NG = len(GROUPS)
    NT = BC * NG
    UNROLL = 3
    S_RING, T_RING, P_RING = 3, 2, 8
    assert NS == NT and NT % P_RING == 0 and (UNROLL * NS) % S_RING == 0 and H % UNROLL == 1

    def offset(c, j):
        return max(0, j - BC * c) * BT

    S_CUTS = [0, 5, 10, 15, 20, 25, 30, 35, 40, 40, 40]

    with ExitStack() as ctx:
        def sb(name, shape, dt=f32):
            return ctx.enter_context(nc.sbuf_tensor(name, shape, dt))

        def sem(name):
            return ctx.enter_context(nc.semaphore(name))

        x_sb = sb("x_sb", [BT, NB, E])
        xT_sb = sb("xT_sb", [E, T])
        wqT_sb = sb("wqT_sb", [E, E])
        wk_sb = sb("wk_sb", [L, E])
        wv_sb = sb("wv_sb", [L, E])
        q2l_sb = sb("q2l_sb", [L, E])
        vup_sb = sb("vup_sb", [L, E])
        wout_sb = sb("wout_sb", [E, E])
        wf_sb = sb("wf_sb", [E, E])
        bias_sb = sb("bias_sb", [BT, E])
        wkh_sb = sb("wkh_sb", [E, E])
        wvh_sb = sb("wvh_sb", [E, E])
        full = sb("full", [E, 2, CW])
        rest = sb("rest", [E, 2, CW])
        q_parts = sb("q_parts", [E, PARTS, T], bf16)
        k_parts = sb("k_parts", [E, PARTS, T], bf16)
        q_aug = sb("q_aug", [AUG, UNROLL, T], bf16)
        k_aug = sb("k_aug", [96, UNROLL, T], bf16)
        v_all = sb("v_all", [BT, NB, E])
        v_head = sb("v_head", [BT, UNROLL, NB, VW])
        probs = sb("probs", [BT, P_RING, CW])
        ctx_sb = sb("ctx_sb", [BT, 2, CW])
        heads = sb("heads", [BT, NB, E])
        tile_max = sb("tile_max", [BT, NB, BC])
        neg_max = sb("neg_max", [BT, NB])
        max_rest = sb("max_rest", [BT, NB])
        max_parts = sb("max_parts", [BT, PARTS, NB], bf16)
        max_rows = sb("max_rows", [PARTS * NB, BT], bf16)
        recip = sb("recip", [BT, NB])
        sel = sb("sel", [BT, D + 1])
        ident_f = sb("ident_f", [BT, BT])
        ident_b = sb("ident_b", [BT, BT], bf16)
        mask = sb("mask", [BT, BT], bf16)
        zero_w = sb("zero_w", [BT, VW], bf16)
        w8 = sb("w8", [E, 2, E], fp8)
        w_t = sb("w_t", [E, 4, E])
        w_q = sb("w_q", [E, E], bf16)
        heads_t = sb("heads_t", [E, 2, CW])
        z = sb("z", [BT, NB, E])
        y = sb("y", [BT, NB, E])
        y8 = sb("y8", [BT, NB, E], fp8)
        y_b = sb("y_b", [BT, NB, E], bf16)
        y_t = sb("y_t", [E, 2, CW], bf16)
        f_h = sb("f_h", [BT, NB, E], f16)
        stats = sb("stats", [BT, 2, NB, 6])
        mv = sb("mv", [BT, 2, NB, 2])
        dev = sb("dev", [BT, 2, NB])
        rstd = sb("rstd", [BT, 2, NB])
        eps = sb("eps", [BT, 1])

        s_bank = [ctx.enter_context(nc.psum_tensor(f"s_bank{n}", [BT, CW], f32)) for n in range(S_RING)]
        t_bank = [ctx.enter_context(nc.psum_tensor(f"t_bank{n}", [BT, CW], f32)) for n in range(T_RING)]
        o_bank = [ctx.enter_context(nc.psum_tensor(f"o_bank{n}", [BT, CW], f32)) for n in range(2)]
        misc = ctx.enter_context(nc.psum_tensor("misc", [BT, CW], f32))
        turned = misc[:, 0:NB * (D + 1)].rearrange("p (b d) -> p b d", d=D + 1)
        max_t = misc[0:PARTS * NB, 256:256 + BT // 2].bitcast(bf16)

        q_dram = nc.dram_tensor("q_parts_dram", [PARTS, E, T], bf16, kind="Internal").ap()
        k_dram = nc.dram_tensor("k_parts_dram", [PARTS, E, T], bf16, kind="Internal").ap()

        x_loaded = sem("x_loaded")
        w_loaded = sem("w_loaded")
        tail_loaded = sem("tail_loaded")
        constants = sem("constants")
        folded = sem("folded")
        folded_sb = sem("folded_sb")
        projected = sem("projected")
        evacuated = sem("evacuated")
        part1 = sem("part1")
        rest_done = sem("rest_done")
        part2 = sem("part2")
        part3 = sem("part3")
        parts_stored = sem("parts_stored")

        def head_sems(name):
            return [sem(f"{name}{b}") for b in range(UNROLL)]

        qk_loaded = head_sems("qk_loaded")
        max_loaded = head_sems("max_loaded")
        s_ready = head_sems("s_ready")
        s_reduced = head_sems("s_reduced")
        max_ready = head_sems("max_ready")
        max_split = head_sems("max_split")
        max_turned = head_sems("max_turned")
        max_copied = head_sems("max_copied")
        t_ready = head_sems("t_ready")
        t_exped = head_sems("t_exped")
        masked = head_sems("masked")
        v_ready = head_sems("v_ready")
        p_used = head_sems("p_used")
        o_copied = head_sems("o_copied")
        ctx_turned = head_sems("ctx_turned")
        normalised = head_sems("normalised")
        HEAD_SEMS = [qk_loaded, max_loaded, s_ready, s_reduced, max_ready, max_split, max_turned, max_copied,
                     t_ready, t_exped, masked, v_ready, p_used, o_copied, ctx_turned, normalised]
        recip_ready = sem("recip_ready")
        t_h = sem("t_h")
        t_hsb = sem("t_hsb")
        t_attn = sem("t_attn")
        t_z = sem("t_z")
        t_stat = sem("t_stat")
        t_mv = sem("t_mv")
        t_dev = sem("t_dev")
        t_rstd = sem("t_rstd")
        t_y = sem("t_y")
        t_y8 = sem("t_y8")
        t_yb = sem("t_yb")
        t_yt = sem("t_yt")
        t_ytsb = sem("t_ytsb")
        t_f = sem("t_f")
        t_fh = sem("t_fh")
        t_w = sem("t_w")
        t_y8b = sem("t_y8b")
        stored = sem("stored")

        CONSTANTS = 10
        QK_LOADS, MAX_LOADS = 16 * PARTS * (PARTS + 1), 16 * PARTS
        block = ctx.enter_context(nc.Block())
        banks = s_bank + t_bank + o_bank

        @block.sync
        def _(sp):
            sp.dma_start(xT_sb[:], xT).then_inc(x_loaded, 16)
            sp.dma_start(wqT_sb[:], wqT).then_inc(w_loaded, 16)
            sp.dma_start(wk_sb[:], wk_down).then_inc(w_loaded, 16)
            sp.dma_start(wv_sb[:], wv_down).then_inc(w_loaded, 16)
            sp.dma_start(q2l_sb[:], q2lT).then_inc(w_loaded, 16)
            sp.dma_start(vup_sb[:], v_upT).then_inc(w_loaded, 16)
            for c in range(NC):
                for n, (src, dst) in enumerate([(q_parts, q_dram), (k_parts, k_dram)]):
                    sp.wait_ge(part3, 2 * c + n + 1)
                    sp.dma_start(dst[:, :, c * CW:(c + 1) * CW].rearrange("p e t -> e p t"),
                                 src[:, :, c * CW:(c + 1) * CW]).then_inc(parts_stored, 16)
            sp.wait_ge(parts_stored, 16 * 2 * NC)

            def load_head(h, b):
                for i in range(PARTS):
                    r = i * PARTS * D
                    sp.dma_start(k_aug[r:r + PARTS * D, b, :],
                                 k_dram[:, bass.ds(h * D, D), :]).then_inc(qk_loaded[b], 16)
                    for j in range(PARTS):
                        sp.dma_start(q_aug[r + j * D:r + j * D + D, b, :],
                                     q_dram[i, bass.ds(h * D, D), :]).then_inc(qk_loaded[b], 16)

            def load_max(b):
                sp.wait_ge(max_copied[b], 1)
                for p in range(PARTS):
                    sp.dma_start(q_aug[ROWS + p:ROWS + p + 1, b, :].rearrange("o (n t) -> o n t", t=BT),
                                 max_rows[p * NB:(p + 1) * NB, :]).then_inc(max_loaded[b], 16)

            sp.wait_ge(constants, CONSTANTS)
            load_head(0, 0)
            load_head(1, 1)
            load_max(0)

            def step(h, b, more):
                nxt, old = (b + 1) % UNROLL, (b + 2) % UNROLL
                if more:
                    sp.wait_ge(o_copied[b], 2)
                    sp.wait_ge(ctx_turned[b], 1)
                    sp.wait_ge(v_ready[nxt], 1)
                    for sems in HEAD_SEMS:
                        sp.sem_clear(sems[old])
                    load_head(h + 2, old)
                load_max(nxt)

            with sp.Fori(0, (H - 1) // UNROLL - 1) as it:
                for k in range(UNROLL):
                    step(it * UNROLL + k, k, True)
            for h in range(H - 1 - UNROLL, H - 1):
                step(h, h % UNROLL, h + 2 < H)
            sp.wait_ge(stored, 16 * NC)

        @block.gpsimd
        def _(pool):
            pool.dma_start(x_sb[:], x.rearrange("(b p) e -> p b e", p=BT)).then_inc(tail_loaded, 16)
            pool.dma_start(wout_sb[:], woutT).then_inc(tail_loaded, 16)
            pool.dma_start(wf_sb[:], ffn_wT).then_inc(tail_loaded, 16)
            pool.dma_start(bias_sb[:], ffn_bias.rearrange("(o e) -> o e", o=1).broadcast_to([BT, E])).then_inc(tail_loaded, 16)

            pool.memset(ident_f[:], 0.0).then_inc(constants, 1)
            pool.wait_ge(constants, 1)
            pool.affine_select(out=ident_f[:], in_=ident_f[:], compare_op=ALU.not_equal, fill=1.0,
                               base=0, pattern=[[-1, BT]], channel_multiplier=1).then_inc(constants, 1)
            pool.wait_ge(constants, 2)
            pool.tensor_copy(ident_b[:], ident_f[:]).then_inc(constants, 1)
            pool.wait_ge(constants, 3)
            pool.memset(mask[:], 0.0).then_inc(constants, 1)
            pool.wait_ge(constants, 4)
            pool.affine_select(out=mask[:], in_=mask[:], compare_op=ALU.is_ge, fill=-1e30,
                               base=0, pattern=[[-1, BT]], channel_multiplier=1).then_inc(constants, 1)
            pool.wait_ge(constants, 5)
            pool.memset(zero_w[:], 0.0).then_inc(constants, 1)
            pool.wait_ge(constants, 6)
            pool.memset(k_aug[64:96, :, :], 1.0).then_inc(constants, 1)
            pool.wait_ge(constants, 7)
            pool.memset(v_head[:], 0.0).then_inc(constants, 1)
            pool.wait_ge(constants, 8)
            pool.memset(v_head[:, :, :, D:D + 1], 1.0).then_inc(constants, 1)
            pool.wait_ge(constants, 9)
            pool.memset(eps[:], EPS).then_inc(constants, 1)
            pool.wait_ge(constants, 10)

            def copy_values(h, b):
                pool.tensor_copy(v_head[:, b, :, 0:D], v_all[:, :, bass.ds(h * D, D)]).then_inc(v_ready[b], 1)

            def split_max(b, first=False):
                done = max_split[b]
                pool.wait_ge(max_ready[b], 1)
                if not first:
                    pool.wait_ge(max_turned[(b + 2) % UNROLL], 1)
                pool.tensor_copy(max_parts[:, 0, :], neg_max[:]).then_inc(done, 1)
                pool.wait_ge(done, 1)
                pool.tensor_tensor(max_rest[:], neg_max[:], max_parts[:, 0, :], ALU.subtract).then_inc(done, 1)
                pool.wait_ge(done, 2)
                pool.tensor_copy(max_parts[:, 1, :], max_rest[:]).then_inc(done, 1)
                pool.wait_ge(done, 3)
                pool.tensor_tensor(max_parts[:, 2, :], max_rest[:], max_parts[:, 1, :], ALU.subtract).then_inc(done, 1)

            def mask_tiles(b, c):
                for q in range(BC):
                    u = BC * GROUPS.index((c, c)) + q
                    pool.wait_ge(t_exped[b], u + 1)
                    d = probs[:, u % P_RING, q * BT:(q + 1) * BT]
                    pool.affine_select(out=d, in_=d, compare_op=ALU.is_ge, fill=0.0, base=0,
                                       pattern=[[1, BT]], channel_multiplier=-1).then_inc(masked[b], 1)

            split_max(0, first=True)
            pool.wait_ge(evacuated, 2 * NC + NC)
            copy_values(0, 0)
            mask_tiles(0, 0)

            def step(h, b, more):
                nxt, old = (b + 1) % UNROLL, (b + 2) % UNROLL
                if more:
                    pool.wait_ge(p_used[old], NT)
                    copy_values(h + 1, nxt)
                for c in range(1, NC - 1):
                    mask_tiles(b, c)
                if more:
                    split_max(nxt)
                mask_tiles(b, NC - 1)
                if more:
                    mask_tiles(nxt, 0)

            with pool.Fori(0, (H - 1) // UNROLL) as it:
                for k in range(UNROLL):
                    step(it * UNROLL + k, k, True)
            step(H - 1, (H - 1) % UNROLL, False)

        @block.scalar
        def _(act):
            for n in range(2 * NC):
                c, is_k = n // 2, n % 2
                parts, scale = (k_parts, 1.0) if is_k else (q_parts, SCALE)
                act.wait_ge(projected, n + 1)
                if n >= 2:
                    act.wait_ge(part3, n - 1)
                act.activation(full[:, n % 2, :], banks[n % 7][:], ACT.Copy, scale=scale).then_inc(part1, 1)
                act.activation(parts[:, 0, c * CW:(c + 1) * CW], banks[n % 7][:], ACT.Copy,
                               scale=scale).then_inc(evacuated, 1)
            for n in range(2 * NC, 3 * NC):
                act.wait_ge(projected, n + 1)
                c = n - 2 * NC
                act.activation(v_all[:, c * BC:(c + 1) * BC, :].rearrange("p b e -> p (b e)"),
                               banks[n % 7][:], ACT.Copy).then_inc(evacuated, 1)

            def exp_group(b, n, first=False):
                c, g = GROUPS[n]
                for q in range(BC):
                    u = BC * n + q
                    o = offset(c, BC * g + q)
                    act.wait_ge(t_ready[b], u + 1)
                    if u >= P_RING:
                        act.wait_ge(p_used[b], u - P_RING + 1)
                    elif not first:
                        act.wait_ge(p_used[(b + 2) % UNROLL], NT + u - P_RING + 1)
                    act.activation(probs[:, u % P_RING, o:CW], t_bank[u % T_RING][:, o:CW],
                                   ACT.Exp).then_inc(t_exped[b], 1)

            def copy_sums(b, c):
                act.wait_ge(p_used[b], BC * (GROUPS.index((c, c)) + 1))
                if c >= 2:
                    act.wait_ge(ctx_turned[b], c - 1)
                else:
                    act.wait_ge(ctx_turned[(b + 2) % UNROLL], NC + c - 1)
                act.activation(ctx_sb[:, c % 2, :], o_bank[c % 2][:], ACT.Copy).then_inc(o_copied[b], 1)

            exp_group(0, 0, first=True)

            def step(b, more):
                for n in range(NG):
                    c, g = GROUPS[n]
                    if n + 1 < NG:
                        exp_group(b, n + 1)
                    if g == c:
                        copy_sums(b, c)
                if more:
                    exp_group((b + 1) % UNROLL, 0)

            with act.Fori(0, (H - 1) // UNROLL) as it:
                for k in range(UNROLL):
                    step(k, True)
            step((H - 1) % UNROLL, False)

            for g in range(NC):
                act.wait_ge(t_h, g + 1)
                if g >= 2:
                    act.wait_ge(t_attn, g - 1)
                act.activation(heads_t[:, g % 2, :], s_bank[g % 2][:], ACT.Copy).then_inc(t_hsb, 1)
            for g in range(NC):
                act.wait_ge(t_mv, g + 1)
                act.activation(dev[:, 0, g * BC:(g + 1) * BC], mv[:, 0, g * BC:(g + 1) * BC, 1], ACT.Sqrt,
                               bias=eps[:]).then_inc(t_dev, 1)
            for g in range(NC):
                act.wait_ge(t_yt, g + 1)
                if g >= 2:
                    act.wait_ge(t_f, g - 1)
                act.activation(y_t[:, g % 2, :], o_bank[g % 2][:, 0:CW // 2].bitcast(bf16), ACT.Copy).then_inc(t_ytsb, 1)
                act.wait_ge(t_f, g + 1)
                act.activation(f_h[:, g * BC:(g + 1) * BC, :].rearrange("p b e -> p (b e)"),
                               t_bank[g % 2][:], ACT.Copy).then_inc(t_fh, 1)
            for g in range(NC):
                act.wait_ge(t_mv, NC + g + 1)
                act.activation(dev[:, 1, g * BC:(g + 1) * BC], mv[:, 1, g * BC:(g + 1) * BC, 1], ACT.Sqrt,
                               bias=eps[:]).then_inc(t_dev, 1)
            for g in range(NC):
                act.wait_ge(t_y, NC + g + 1)
                act.dma_start(out[g * CW:(g + 1) * CW, :].rearrange("(b p) e -> p b e", p=BT),
                              z[:, g * BC:(g + 1) * BC, :]).then_inc(stored, 16)

        @block.tensor
        def _(pe):
            pe.wait_ge(w_loaded, 16 * 5)
            pe.matmul(misc[:, 0:E], wk_sb[:], q2l_sb[:], start=True, stop=True)
            pe.matmul(misc[:, E:2 * E], wv_sb[:], vup_sb[:], start=True, stop=True).then_inc(folded, 1)
            pe.wait_ge(x_loaded, 16)
            for n in range(3 * NC):
                if n == 1:
                    pe.wait_ge(folded_sb, 1)
                if n >= 7:
                    pe.wait_ge(evacuated, n - 6)
                if n < 2 * NC:
                    c = n // 2
                    w = wkh_sb if n % 2 else wqT_sb
                    mm = pe.matmul(banks[n % 7][:], w[:], xT_sb[:, c * CW:(c + 1) * CW], start=True, stop=True)
                else:
                    c = n - 2 * NC
                    for b in range(BC):
                        t = c * CW + b * BT
                        mm = pe.matmul(banks[n % 7][:, b * BT:(b + 1) * BT], xT_sb[:, t:t + BT], wvh_sb[:],
                                       start=True, stop=True)
                mm.then_inc(projected, 1)

            def max_tile(b, u, ring, first=False):
                i, c, w = S_TILES[u]
                diagonal = c == i // BC
                bank = s_bank[ring]
                if u >= S_RING:
                    pe.wait_ge(s_reduced[b], u - S_RING + 1)
                elif not first:
                    pe.wait_ge(s_reduced[(b + 2) % UNROLL], NS + u - S_RING + 1)
                mm = pe.matmul(bank[:, 0:w], q_aug[0:ROWS, b, i * BT:(i + 1) * BT],
                               k_aug[0:ROWS, b, c * CW:c * CW + w], start=True, stop=not diagonal)
                if diagonal:
                    mm = pe.matmul(bank[:, w - BT:w], ident_b[:], mask[:], start=False, stop=True)
                mm.then_inc(s_ready[b], 1)

            def score_tile(b, n, q, first=False):
                c, g = GROUPS[n]
                j = BC * g + q
                o = offset(c, j)
                u = BC * n + q
                if u >= T_RING:
                    pe.wait_ge(t_exped[b], u - T_RING + 1)
                elif not first:
                    pe.wait_ge(t_exped[(b + 2) % UNROLL], NT + u - T_RING + 1)
                pe.matmul(t_bank[u % T_RING][:, o:CW], k_aug[0:AUG, b, j * BT:(j + 1) * BT],
                          q_aug[0:AUG, b, c * CW + o:(c + 1) * CW], start=True, stop=True).then_inc(t_ready[b], 1)

            def value_group(b, n):
                c, g = GROUPS[n]
                if g == 0 and c >= 2:
                    pe.wait_ge(o_copied[b], c - 1)
                elif g == 0:
                    pe.wait_ge(o_copied[(b + 2) % UNROLL], NC + c - 1)
                if g == 0 and c == 0:
                    for q in range(1, BC):
                        pe.matmul(o_bank[0][q * VW:(q + 1) * VW, :], zero_w[:], q_parts[:, 0, 0:CW],
                                  start=True, stop=False)
                for q in range(BC):
                    j = BC * g + q
                    o = offset(c, j)
                    u = BC * n + q
                    if g == c:
                        pe.wait_ge(masked[b], c * BC + q + 1)
                    else:
                        pe.wait_ge(t_exped[b], u + 1)
                    mm = pe.matmul(o_bank[c % 2][q * VW:(q + 1) * VW, o:CW], v_head[:, b, j, :],
                                   probs[:, u % P_RING, o:CW], start=g == 0 and (c > 0 or q == 0), stop=g == c)
                mm.then_inc(p_used[b], BC)

            def turn_sums(b, c):
                if c == 0:
                    pe.wait_ge(normalised[(b + 2) % UNROLL], 1)
                pe.wait_ge(o_copied[b], c + 1)
                for t in range(BC):
                    mm = pe.matmul(turned[:, c * BC + t, :], ctx_sb[:, c % 2, t * BT:(t + 1) * BT], sel[:],
                                   start=True, stop=True)
                mm.then_inc(ctx_turned[b], 1)

            def turn_max(b):
                pe.wait_ge(max_split[b], 4)
                pe.transpose(max_t, max_parts[:].rearrange("p a b -> p (a b)"), ident_b[:]).then_inc(max_turned[b], 1)

            pe.wait_ge(evacuated, 3 * NC)
            pe.wait_ge(qk_loaded[0], QK_LOADS)
            for u in range(NS):
                max_tile(0, u, u % S_RING, first=True)
            turn_max(0)
            pe.wait_ge(max_loaded[0], MAX_LOADS)
            for q in range(BC):
                score_tile(0, 0, q, first=True)

            TURN_AFTER = {1: 0, 3: 1, 6: 2}

            def step(b, more):
                nxt = (b + 1) % UNROLL
                pe.wait_ge(v_ready[b], 1)
                if more:
                    pe.wait_ge(qk_loaded[nxt], QK_LOADS)
                for n in range(NG):
                    if n + 1 < NG:
                        for q in range(BC):
                            score_tile(b, n + 1, q)
                            if more:
                                lo, hi = S_CUTS[n], S_CUTS[n + 1]
                                for u in range(lo + (hi - lo) * q // BC, lo + (hi - lo) * (q + 1) // BC):
                                    max_tile(nxt, u, (nxt * NS + u) % S_RING)
                    value_group(b, n)
                    if n in TURN_AFTER:
                        turn_sums(b, TURN_AFTER[n])
                    if n == NG - 2 and more:
                        turn_max(nxt)
                if more:
                    pe.wait_ge(max_loaded[nxt], MAX_LOADS)
                    for q in range(BC):
                        score_tile(nxt, 0, q)
                    pe.wait_ge(max_copied[nxt], 1)
                turn_sums(b, NC - 1)

            with pe.Fori(0, (H - 1) // UNROLL) as it:
                for k in range(UNROLL):
                    step(k, True)
            step((H - 1) % UNROLL, False)

            for g in range(NC):
                pe.wait_ge(normalised[(H - 1) % UNROLL], 1)
                if g >= 2:
                    pe.wait_ge(t_hsb, g - 1)
                for b in range(BC):
                    mm = pe.transpose(s_bank[g % 2][:, b * BT:(b + 1) * BT], heads[:, g * BC + b, :], ident_f[:])
                mm.then_inc(t_h, 1)
                pe.wait_ge(t_hsb, g + 1)
                if g >= 2:
                    pe.wait_ge(t_z, g - 1)
                if g == 0:
                    pe.wait_ge(tail_loaded, 64)
                for b in range(BC):
                    mm = pe.matmul(t_bank[g % 2][:, b * BT:(b + 1) * BT], heads_t[:, g % 2, b * BT:(b + 1) * BT],
                                   wout_sb[:], start=True, stop=True)
                mm.then_inc(t_attn, 1)
            pe.wait_ge(t_w, 11)
            for g in range(NC):
                pe.wait_ge(t_yb, g + 1)
                if g >= 2:
                    pe.wait_ge(t_ytsb, g - 1)
                for b in range(BC):
                    mm = pe.transpose(o_bank[g % 2][:, b * BT // 2:(b + 1) * BT // 2].bitcast(bf16),
                                      y_b[:, g * BC + b, :], ident_b[:])
                mm.then_inc(t_yt, 1)
                pe.wait_ge(t_ytsb, g + 1)
                if g < 2:
                    pe.wait_ge(t_z, NC)
                else:
                    pe.wait_ge(t_fh, g - 1)
                for b in range(BC):
                    mm = pe.matmul(t_bank[g % 2][:, b * BT:(b + 1) * BT], y_t[:, g % 2, b * BT:(b + 1) * BT],
                                   w_q[:], start=True, stop=True)
                mm.then_inc(t_f, 1)

        @block.vector
        def _(dve):
            last = UNROLL - 1
            dve.memset(tile_max[:], -3.0e38).then_inc(p_used[last], NT)
            dve.memset(rstd[:, 0, :], 0.0).then_inc(o_copied[last], NC)
            dve.memset(rstd[:, 1, :], 0.0).then_inc(ctx_turned[last], NC)
            dve.memset(recip[:], 0.0).then_inc(normalised[last], 1)
            dve.wait_ge(constants, 2)
            dve.tensor_reduce(sel[:], ident_f[:].rearrange("p (q r) -> p r q", q=4)[:, 0:D + 1, :], AX.X,
                              ALU.add).then_inc(t_w, 1)
            dve.wait_ge(folded, 1)
            dve.tensor_copy(wkh_sb[:], misc[:, 0:E]).then_inc(t_w, 1)
            dve.wait_ge(t_w, 2)
            dve.tensor_copy(wvh_sb[:], misc[:, E:2 * E]).then_inc(folded_sb, 1)
            for n in range(2 * NC):
                c = n // 2
                parts = k_parts if n % 2 else q_parts
                cs = slice(c * CW, (c + 1) * CW)
                dve.wait_ge(evacuated, n + 1)
                dve.tensor_tensor(rest[:, n % 2, :], full[:, n % 2, :], parts[:, 0, cs],
                                  ALU.subtract).then_inc(rest_done, 1)
                dve.wait_ge(rest_done, n + 1)
                dve.tensor_copy(parts[:, 1, cs], rest[:, n % 2, :]).then_inc(part2, 1)
                dve.wait_ge(part2, n + 1)
                dve.tensor_tensor(parts[:, 2, cs], rest[:, n % 2, :], parts[:, 1, cs],
                                  ALU.subtract).then_inc(part3, 1)

            def reduce_tile(b, u):
                i, c, w = S_TILES[u]
                dve.wait_ge(s_ready[b], u + 1)
                dve.tensor_reduce(tile_max[:, i, c:c + 1], s_bank[(b * NS + u) % S_RING][:, 0:w], AX.X,
                                  ALU.max).then_inc(s_reduced[b], 1)

            def finish_max(b, first=False):
                dve.wait_ge(s_reduced[b], NS)
                dve.tensor_reduce(neg_max[:], tile_max[:], AX.X, ALU.max, negate=True).then_inc(max_ready[b], 1)
                if not first:
                    dve.wait_ge(max_loaded[(b + 2) % UNROLL], MAX_LOADS)
                dve.wait_ge(max_turned[b], 1)
                dve.tensor_copy(max_rows[:], max_t).then_inc(max_copied[b], 1)

            def normalise(h, b):
                dve.wait_ge(ctx_turned[b], NC)
                dve.reciprocal(recip[:], turned[:, :, D]).then_inc(recip_ready, 1)
                dve.wait_ge(recip_ready, 1)
                dve.sem_clear(recip_ready)
                dve.tensor_tensor(heads[:, :, bass.ds(h * D, D)], turned[:, :, 0:D],
                                  recip[:].rearrange("p (b o) -> p b o", o=1).broadcast_to([BT, NB, D]),
                                  ALU.mult).then_inc(normalised[b], 1)

            for u in range(NS):
                reduce_tile(0, u)
            finish_max(0, first=True)

            with dve.Fori(0, (H - 1) // UNROLL) as it:
                for k in range(UNROLL):
                    nxt = (k + 1) % UNROLL
                    for u in range(NS):
                        reduce_tile(nxt, u)
                    finish_max(nxt)
                    normalise(it * UNROLL + k, k)
            normalise(H - 1, (H - 1) % UNROLL)

            t_done = [2]

            def w_step(ins):
                ins.then_inc(t_w, 1)
                t_done[0] += 1
                dve.wait_ge(t_w, t_done[0])

            dve.wait_ge(tail_loaded, 64)
            w_step(dve.tensor_scalar(w_t[:, 0, :], wf_sb[:], 448.0, -448.0, ALU.min, ALU.max))
            w_step(dve.tensor_scalar(w_t[:, 1, :], wf_sb[:], 240.0, -240.0, ALU.min, ALU.max))
            w_step(dve.tensor_scalar(w8[:, 0, :], w_t[:, 1, :], 1.0, None, ALU.mult, saturate=False))
            w_step(dve.tensor_scalar(w8[:, 1, :], w_t[:, 0, :], 0.5, None, ALU.mult, saturate=False))
            w_step(dve.tensor_tensor(w_t[:, 2, :], w_t[:, 0, :], w_t[:, 0, :], ALU.mult))
            w_step(dve.tensor_scalar(w_t[:, 2, :], w_t[:, 2, :], 128.0 ** 2, None, ALU.is_ge))
            w_step(dve.scalar_tensor_tensor(out=w_t[:, 3, :], in0=w8[:, 1, :], scalar=2.0, in1=w8[:, 0, :],
                                            op0=ALU.mult, op1=ALU.subtract))
            w_step(dve.tensor_tensor(w_t[:, 1, :], w_t[:, 3, :], w_t[:, 2, :], ALU.mult))
            dve.tensor_tensor(w_q[:], w_t[:, 1, :], w8[:, 0, :], ALU.add).then_inc(t_w, 1)

            def layernorm(which, g, src, dst):
                base = which * NB + g * BC
                for b in range(g * BC, (g + 1) * BC):
                    dve.bn_stats(stats[:, which, b, :], src[:, b, :]).then_inc(t_stat, 1)
                for b in range(g * BC, (g + 1) * BC):
                    dve.wait_ge(t_stat, which * NB + b + 1)
                    ins = dve.bn_aggr(mv[:, which, b, :], stats[:, which, b, :])
                ins.then_inc(t_mv, 1)

            def normal(which, g, src, dst):
                gs = slice(g * BC, (g + 1) * BC)
                dve.wait_ge(t_dev, which * NC + g + 1)
                dve.reciprocal(rstd[:, which, gs], dev[:, which, gs]).then_inc(t_rstd, 1)
                dve.wait_ge(t_rstd, which * NC + g + 1)
                dve.wait_ge(t_mv, which * NC + g + 1)
                for b in range(g * BC, (g + 1) * BC):
                    ins = dve.tensor_scalar(dst[:, b, :], src[:, b, :], mv[:, which, b, 0:1], rstd[:, which, b:b + 1],
                                            ALU.subtract, ALU.mult)
                ins.then_inc(t_y, 1)

            for g in range(NC):
                gs = slice(g * BC, (g + 1) * BC)
                dve.wait_ge(t_attn, g + 1)
                dve.tensor_tensor(z[:, gs, :].rearrange("p b e -> p (b e)"), t_bank[g % 2][:],
                                  x_sb[:, gs, :].rearrange("p b e -> p (b e)"), ALU.add).then_inc(t_z, 1)
                dve.wait_ge(t_z, g + 1)
                layernorm(0, g, z, y)
            for g in range(NC):
                gs = slice(g * BC, (g + 1) * BC)
                normal(0, g, z, y)
                dve.wait_ge(t_y, g + 1)
                dve.tensor_copy(y8[:, gs, :], y[:, gs, :], saturate=False).then_inc(t_y8, 1)
                dve.wait_ge(t_y8, g + 1)
                dve.tensor_copy(y_b[:, gs, :], y8[:, gs, :]).then_inc(t_yb, 1)
                for b in range(g * BC, (g + 1) * BC):
                    ins = dve.tensor_tensor(y[:, b, :], y[:, b, :], bias_sb[:], ALU.add)
                ins.then_inc(t_y8b, 1)
            for g in range(NC):
                gs = slice(g * BC, (g + 1) * BC)
                dve.wait_ge(t_fh, g + 1)
                dve.wait_ge(t_y8b, g + 1)
                dve.tensor_tensor(y[:, gs, :], y[:, gs, :], f_h[:, gs, :], ALU.add).then_inc(t_z, 1)
                dve.wait_ge(t_z, NC + g + 1)
                layernorm(1, g, y, z)
            for g in range(NC):
                normal(1, g, y, z)


_INS = ["x", "xT", "wqT", "wk_down", "wv_down", "q2lT", "v_upT", "woutT", "ffn_wT", "ffn_bias"]


def kernel(L0_attn_hidden_states, L0_attn_Wq, L0_attn_Wk_down, L0_attn_Wv_down, L0_attn_q_to_latent,
           L0_attn_v_up, L0_attn_Wout, L0_ffn_weight, L0_ffn_bias):
    import numpy as np
    import concourse.bacc as bacc
    from concourse import mybir as _mybir
    from concourse.bass_utils import run_bass_kernel_spmd

    x = np.asarray(L0_attn_hidden_states)[0]
    T, E = x.shape
    H, D, L = L0_attn_q_to_latent.shape
    laid = {
        "x": x,
        "xT": x.T,
        "wqT": np.asarray(L0_attn_Wq).T,
        "wk_down": np.asarray(L0_attn_Wk_down),
        "wv_down": np.asarray(L0_attn_Wv_down),
        "q2lT": np.asarray(L0_attn_q_to_latent).reshape(H * D, L).T,
        "v_upT": np.asarray(L0_attn_v_up).transpose(1, 0, 2).reshape(L, H * D),
        "woutT": np.asarray(L0_attn_Wout).T,
        "ffn_wT": np.asarray(L0_ffn_weight).T,
        "ffn_bias": np.asarray(L0_ffn_bias),
    }
    nc = bacc.Bacc("TRN2", target_bir_lowering=False, num_devices=1)
    arrays, args = {}, []
    for name in _INS:
        a = np.ascontiguousarray(laid[name])
        arrays[f"in_{name}"] = a
        args.append(nc.dram_tensor(f"in_{name}", a.shape, _mybir.dt.from_np(a.dtype), kind="ExternalInput").ap())
    out = nc.dram_tensor("out", (T, E), _mybir.dt.from_np(x.dtype), kind="ExternalOutput").ap()
    postln_block_kernel(nc, *args, out)
    r = run_bass_kernel_spmd(nc, [arrays], core_ids=[0])
    return r.results[0]["out"].reshape(1, T, E)
```

```python
import concourse.bass as bass
from concourse import mybir
from contextlib import ExitStack


def postln_block_kernel(nc, x, xT, wqT, wk_down, wv_down, q2lT, v_upT, woutT, ffn_wT, ffn_bias, out):
    f32, bf16, f16 = mybir.dt.float32, mybir.dt.bfloat16, mybir.dt.float16
    fp8 = mybir.dt.float8e4
    ALU, ACT, AX = mybir.AluOpType, mybir.ActivationFunctionType, mybir.AxisListType

    T, E = x.shape
    L = wk_down.shape[0]
    H = 16
    D = E // H
    BT = 128
    NB = T // BT
    CW = 512
    NC = T // CW
    BC = CW // BT
    PARTS = 3
    ROWS = PARTS * PARTS * D
    PAD = 96
    AUG = 128
    VW = 32
    SCALE = 1.0 / 8.0
    EPS = 1e-5
    assert L == 64 and ROWS == 72

    S_TILES = [(i, c, min(CW, (i + 1) * BT - c * CW)) for i in range(NB) for c in range(i // BC + 1)]
    NS = len(S_TILES)
    GROUPS = [[j] for j in range(2 * BC)] + [[8, 9], [10, 11], [12, 13, 14, 15]]
    NG = len(GROUPS)

    def tiles_of(js):
        out = []
        for n, j in enumerate(js):
            c0 = j // BC
            for c in range(c0, NC):
                o = (j - BC * c0) * BT if c == c0 else 0
                out.append((j, c, o, (n * (NC - c0) + c - c0) * CW))
        return out

    TILES = [tiles_of(js) for js in GROUPS]
    FIRST = [sum(len(t) for t in TILES[:n]) for n in range(NG + 1)]
    NT = FIRST[NG]
    UNROLL = 3
    S_RING, T_RING, P_RING = 3, 3, 3
    EARLY = 20
    assert NS == NT and H % UNROLL == 1 and sorted(sum(GROUPS, [])) == list(range(NB))

    with ExitStack() as ctx:
        def sb(name, shape, dt=f32):
            return ctx.enter_context(nc.sbuf_tensor(name, shape, dt))

        def sem(name):
            return ctx.enter_context(nc.semaphore(name))

        x_sb = sb("x_sb", [BT, NB, E])
        xT_sb = sb("xT_sb", [E, T])
        wqT_sb = sb("wqT_sb", [E, E])
        wk_sb = sb("wk_sb", [L, E])
        wv_sb = sb("wv_sb", [L, E])
        q2l_sb = sb("q2l_sb", [L, E])
        vup_sb = sb("vup_sb", [L, E])
        wout_sb = sb("wout_sb", [E, E])
        wf_sb = sb("wf_sb", [E, E])
        bias_sb = sb("bias_sb", [BT, E])
        wkh_sb = sb("wkh_sb", [E, E])
        wvh_sb = sb("wvh_sb", [E, E])
        full = sb("full", [E, 2, CW])
        rest = sb("rest", [E, 2, CW])
        q_parts = sb("q_parts", [E, PARTS, T], bf16)
        k_parts = sb("k_parts", [E, PARTS, T], bf16)
        q_aug = sb("q_aug", [AUG, UNROLL, T], bf16)
        k_aug = sb("k_aug", [AUG, UNROLL, T], bf16)
        v_all = sb("v_all", [BT, NB, E])
        v_head = sb("v_head", [BT, UNROLL, NB, VW])
        probs = sb("probs", [BT, P_RING, T])
        ctx_sb = sb("ctx_sb", [BT, CW])
        heads = sb("heads", [BT, NB, E])
        tile_max = sb("tile_max", [BT, UNROLL, NB, BC])
        neg_max = sb("neg_max", [BT, NB])
        max_rest = sb("max_rest", [BT, NB])
        max_parts = sb("max_parts", [BT, PARTS, NB], bf16)
        max_rows = sb("max_rows", [PARTS * NB, BT], bf16)
        recip = sb("recip", [BT, NB])
        sel = sb("sel", [BT, BC, D + 1])
        ident_f = sb("ident_f", [BT, BT])
        ident_b = sb("ident_b", [BT, BT], bf16)
        mask = sb("mask", [BT, BT], bf16)
        w8 = sb("w8", [E, 2, E], fp8)
        w_t = sb("w_t", [E, 4, E])
        w_q = sb("w_q", [E, E], bf16)
        heads_t = sb("heads_t", [E, 2, CW])
        z = sb("z", [BT, NB, E])
        y = sb("y", [BT, NB, E])
        y8 = sb("y8", [BT, NB, E], fp8)
        y_b = sb("y_b", [BT, NB, E], bf16)
        y_t = sb("y_t", [E, 2, CW], bf16)
        f_h = sb("f_h", [BT, NB, E], f16)
        stats = sb("stats", [BT, 2, NB, 6])
        mv = sb("mv", [BT, 2, NB, 2])
        dev = sb("dev", [BT, 2, NB])
        rstd = sb("rstd", [BT, 2, NB])
        eps = sb("eps", [BT, 1])

        s_bank = [ctx.enter_context(nc.psum_tensor(f"s_bank{n}", [BT, CW], f32)) for n in range(S_RING)]
        t_bank = [ctx.enter_context(nc.psum_tensor(f"t_bank{n}", [BT, CW], f32)) for n in range(T_RING)]
        o_bank = ctx.enter_context(nc.psum_tensor("o_bank", [BT, CW], f32))
        misc = ctx.enter_context(nc.psum_tensor("misc", [BT, CW], f32))
        turned = misc[:, 0:NB * (D + 1)].rearrange("p (b d) -> p b d", d=D + 1)
        max_t = misc[0:PARTS * NB, 256:256 + BT // 2].bitcast(bf16)

        q_dram = nc.dram_tensor("q_parts_dram", [PARTS, E, T], bf16, kind="Internal").ap()
        k_dram = nc.dram_tensor("k_parts_dram", [H, PARTS * D, T], bf16, kind="Internal").ap()

        x_loaded = sem("x_loaded")
        w_loaded = sem("w_loaded")
        tail_loaded = sem("tail_loaded")
        constants = sem("constants")
        folded = sem("folded")
        folded_sb = sem("folded_sb")
        projected = sem("projected")
        evacuated = sem("evacuated")
        part1 = sem("part1")
        rest_done = sem("rest_done")
        part2 = sem("part2")
        part3 = sem("part3")
        parts_stored = sem("parts_stored")

        def head_sems(name):
            return [sem(f"{name}{b}") for b in range(UNROLL)]

        qk_loaded = head_sems("qk_loaded")
        max_loaded = head_sems("max_loaded")
        s_ready = head_sems("s_ready")
        s_reduced = head_sems("s_reduced")
        max_ready = head_sems("max_ready")
        max_split = head_sems("max_split")
        max_turned = head_sems("max_turned")
        max_copied = head_sems("max_copied")
        t_ready = head_sems("t_ready")
        t_exped = head_sems("t_exped")
        masked = head_sems("masked")
        v_ready = head_sems("v_ready")
        p_used = head_sems("p_used")
        o_copied = head_sems("o_copied")
        ctx_turned = head_sems("ctx_turned")
        normalised = head_sems("normalised")
        cleared = head_sems("cleared")
        HEAD_SEMS = [cleared, qk_loaded, max_loaded, s_ready, s_reduced, max_ready, max_split, max_turned, max_copied,
                     t_ready, t_exped, masked, v_ready, p_used, o_copied, ctx_turned, normalised]
        recip_ready = sem("recip_ready")
        t_h = sem("t_h")
        t_hsb = sem("t_hsb")
        t_attn = sem("t_attn")
        t_z = sem("t_z")
        t_stat = sem("t_stat")
        t_mv = sem("t_mv")
        t_dev = sem("t_dev")
        t_rstd = sem("t_rstd")
        t_y = sem("t_y")
        t_y8 = sem("t_y8")
        t_yb = sem("t_yb")
        t_yt = sem("t_yt")
        t_ytsb = sem("t_ytsb")
        t_f = sem("t_f")
        t_fh = sem("t_fh")
        t_w = sem("t_w")
        t_y8b = sem("t_y8b")
        stored = sem("stored")

        CONSTANTS = 11
        LOOPS = (H - 2) // UNROLL
        QK_LOADS, MAX_LOADS = 16 * 2 * PARTS, 16
        SPLIT_AFTER, TURN_MAX_AFTER = 7, 9
        block = ctx.enter_context(nc.Block())
        banks = s_bank + t_bank + [o_bank]

        @block.sync
        def _(sp):
            sp.dma_start(xT_sb[:], xT).then_inc(x_loaded, 16)
            sp.dma_start(wqT_sb[:], wqT).then_inc(w_loaded, 16)
            sp.dma_start(wk_sb[:], wk_down).then_inc(w_loaded, 16)
            sp.dma_start(wv_sb[:], wv_down).then_inc(w_loaded, 16)
            sp.dma_start(q2l_sb[:], q2lT).then_inc(w_loaded, 16)
            sp.dma_start(vup_sb[:], v_upT).then_inc(w_loaded, 16)
            for c in range(NC):
                cs = slice(c * CW, (c + 1) * CW)
                sp.wait_ge(part3, 2 * c + 1)
                sp.dma_start(q_dram[:, :, cs].rearrange("p e t -> e p t"),
                             q_parts[:, :, cs]).then_inc(parts_stored, 16)
                sp.wait_ge(part3, 2 * c + 2)
                for p in range(PARTS):
                    sp.dma_start(k_dram[:, p * D:(p + 1) * D, cs], k_parts[:, p, cs]).then_inc(parts_stored, 16)
            sp.wait_ge(parts_stored, 16 * 4 * NC)

            def load_head(h, b):
                for i in range(PARTS):
                    r = i * PARTS * D
                    sp.dma_start(k_aug[r:r + PARTS * D, b, :], k_dram[h, :, :]).then_inc(qk_loaded[b], 16)
                    q_rows = q_dram[i, bass.ds(h * D, D), :].rearrange("(o d) t -> o d t", o=1)
                    sp.dma_start(q_aug[r:r + PARTS * D, b, :],
                                 q_rows.broadcast_to([PARTS, D, T])).then_inc(qk_loaded[b], 16)

            def load_max(b):
                sp.wait_ge(max_copied[b], 1)
                sp.dma_start(q_aug[PAD:PAD + PARTS, b, :], max_rows[:]).then_inc(max_loaded[b], 16)

            sp.wait_ge(constants, CONSTANTS)
            load_head(0, 0)
            load_head(1, 1)
            load_max(0)

            def step(h, b, more):
                nxt, old = (b + 1) % UNROLL, (b + 2) % UNROLL
                if more:
                    sp.wait_ge(t_exped[b], FIRST[2] + 1)
                    sp.wait_ge(p_used[b], 2)
                    sp.wait_ge(v_ready[nxt], 1)
                    for sems in HEAD_SEMS:
                        sp.sem_clear(sems[old])
                    sp.sem_inc(cleared[b], 1)
                    load_head(h + 2, old)
                load_max(nxt)

            with sp.Fori(0, (H - 1) // UNROLL - 1) as it:
                for k in range(UNROLL):
                    step(it * UNROLL + k, k, True)
            for h in range(H - 1 - UNROLL, H - 1):
                step(h, h % UNROLL, h + 2 < H)
            sp.wait_ge(stored, 16 * NC)

        @block.gpsimd
        def _(pool):
            pool.dma_start(x_sb[:], x.rearrange("(b p) e -> p b e", p=BT)).then_inc(tail_loaded, 16)
            pool.dma_start(wout_sb[:], woutT).then_inc(tail_loaded, 16)
            pool.dma_start(wf_sb[:], ffn_wT).then_inc(tail_loaded, 16)
            pool.dma_start(bias_sb[:], ffn_bias.rearrange("(o e) -> o e", o=1).broadcast_to([BT, E])).then_inc(tail_loaded, 16)

            pool.memset(ident_f[:], 0.0).then_inc(constants, 1)
            pool.wait_ge(constants, 1)
            pool.affine_select(out=ident_f[:], in_=ident_f[:], compare_op=ALU.not_equal, fill=1.0,
                               base=0, pattern=[[-1, BT]], channel_multiplier=1).then_inc(constants, 1)
            pool.wait_ge(constants, 2)
            pool.tensor_copy(ident_b[:], ident_f[:]).then_inc(constants, 1)
            pool.wait_ge(constants, 3)
            pool.memset(mask[:], 0.0).then_inc(constants, 1)
            pool.wait_ge(constants, 4)
            pool.affine_select(out=mask[:], in_=mask[:], compare_op=ALU.is_ge, fill=-1e30,
                               base=0, pattern=[[-1, BT]], channel_multiplier=1).then_inc(constants, 1)
            pool.wait_ge(constants, 5)
            pool.memset(q_aug[64:128, :, :], 0.0).then_inc(constants, 1)
            pool.wait_ge(constants, 6)
            pool.memset(k_aug[64:128, :, :], 0.0).then_inc(constants, 1)
            pool.wait_ge(constants, 7)
            pool.memset(k_aug[PAD:128, :, :], 1.0).then_inc(constants, 1)
            pool.wait_ge(constants, 8)
            pool.memset(v_head[:], 0.0).then_inc(constants, 1)
            pool.wait_ge(constants, 9)
            pool.memset(v_head[:, :, :, D:D + 1], 1.0).then_inc(constants, 1)
            pool.wait_ge(constants, 10)
            pool.memset(eps[:], EPS).then_inc(constants, 1)
            pool.wait_ge(constants, 11)

            def copy_values(h, b):
                pool.tensor_copy(v_head[:, b, :, 0:D], v_all[:, :, bass.ds(h * D, D)]).then_inc(v_ready[b], 1)

            def split_max(b, first=False):
                done = max_split[b]
                pool.wait_ge(max_ready[b], 1)
                if not first:
                    pool.wait_ge(max_turned[(b + 2) % UNROLL], 1)
                pool.tensor_copy(max_parts[:, 0, :], neg_max[:]).then_inc(done, 1)
                pool.wait_ge(done, 1)
                pool.tensor_tensor(max_rest[:], neg_max[:], max_parts[:, 0, :], ALU.subtract).then_inc(done, 1)
                pool.wait_ge(done, 2)
                pool.tensor_copy(max_parts[:, 1, :], max_rest[:]).then_inc(done, 1)
                pool.wait_ge(done, 3)
                pool.tensor_tensor(max_parts[:, 2, :], max_rest[:], max_parts[:, 1, :], ALU.subtract).then_inc(done, 1)

            def mask_group(b, n):
                for k, (j, c, o, col) in enumerate(TILES[n]):
                    if c == j // BC:
                        pool.wait_ge(t_exped[b], FIRST[n] + k + 1)
                        d = probs[:, (b * NG + n) % P_RING, col + o:col + o + BT]
                        pool.affine_select(out=d, in_=d, compare_op=ALU.is_ge, fill=0.0, base=0,
                                           pattern=[[1, BT]], channel_multiplier=-1).then_inc(masked[b], 1)

            split_max(0, first=True)
            pool.wait_ge(evacuated, 2 * NC + NC)
            copy_values(0, 0)
            mask_group(0, 0)
            mask_group(0, 1)

            def step(h, b, more):
                nxt, old = (b + 1) % UNROLL, (b + 2) % UNROLL
                if more:
                    pool.wait_ge(p_used[old], NG)
                    copy_values(h + 1, nxt)
                for n in range(2, NG):
                    mask_group(b, n)
                    if more and n == SPLIT_AFTER:
                        split_max(nxt)
                if more:
                    mask_group(nxt, 0)
                    mask_group(nxt, 1)

            with pool.Fori(0, (H - 1) // UNROLL) as it:
                for k in range(UNROLL):
                    step(it * UNROLL + k, k, True)
            step(H - 1, (H - 1) % UNROLL, False)

        @block.scalar
        def _(act):
            for n in range(2 * NC):
                c, is_k = n // 2, n % 2
                parts, scale = (k_parts, 1.0) if is_k else (q_parts, SCALE)
                act.wait_ge(projected, n + 1)
                if n >= 2:
                    act.wait_ge(part3, n - 1)
                act.activation(full[:, n % 2, :], banks[n % 7][:], ACT.Copy, scale=scale).then_inc(part1, 1)
                act.activation(parts[:, 0, c * CW:(c + 1) * CW], banks[n % 7][:], ACT.Copy,
                               scale=scale).then_inc(evacuated, 1)
            for n in range(2 * NC, 3 * NC):
                act.wait_ge(projected, n + 1)
                c = n - 2 * NC
                act.activation(v_all[:, c * BC:(c + 1) * BC, :].rearrange("p b e -> p (b e)"),
                               banks[n % 7][:], ACT.Copy).then_inc(evacuated, 1)

            def exp_group(b, n, first=False):
                if n >= P_RING:
                    act.wait_ge(p_used[b], n - P_RING + 1)
                elif not first:
                    act.wait_ge(p_used[(b + 2) % UNROLL], NG + n - P_RING + 1)
                for k, (j, c, o, col) in enumerate(TILES[n]):
                    u = FIRST[n] + k
                    act.wait_ge(t_ready[b], u + 1)
                    act.activation(probs[:, (b * NG + n) % P_RING, col + o:col + CW],
                                   t_bank[(b * NT + u) % T_RING][:, o:CW], ACT.Exp).then_inc(t_exped[b], 1)

            def copy_sums(b):
                act.wait_ge(p_used[b], NG)
                act.activation(ctx_sb[:], o_bank[:], ACT.Copy).then_inc(o_copied[b], 1)

            exp_group(0, 0, first=True)
            exp_group(0, 1, first=True)

            def step(b, more, first=False):
                nxt = (b + 1) % UNROLL
                for n in range(2, NG):
                    exp_group(b, n)
                if more:
                    exp_group(nxt, 0)
                copy_sums(b)
                if more:
                    exp_group(nxt, 1)

            with act.Fori(0, (H - 1) // UNROLL) as it:
                for k in range(UNROLL):
                    step(k, True)
            step((H - 1) % UNROLL, False)

            for g in range(NC):
                act.wait_ge(t_h, g + 1)
                if g >= 2:
                    act.wait_ge(t_attn, g - 1)
                act.activation(heads_t[:, g % 2, :], s_bank[g % 2][:], ACT.Copy).then_inc(t_hsb, 1)
            for g in range(NC):
                act.wait_ge(t_mv, g + 1)
                act.activation(dev[:, 0, g * BC:(g + 1) * BC], mv[:, 0, g * BC:(g + 1) * BC, 1], ACT.Sqrt,
                               bias=eps[:]).then_inc(t_dev, 1)
            for g in range(NC):
                act.wait_ge(t_yt, g + 1)
                if g >= 2:
                    act.wait_ge(t_f, g - 1)
                act.activation(y_t[:, g % 2, :], s_bank[g % 2][:, 0:CW // 2].bitcast(bf16), ACT.Copy).then_inc(t_ytsb, 1)
                act.wait_ge(t_f, g + 1)
                act.activation(f_h[:, g * BC:(g + 1) * BC, :].rearrange("p b e -> p (b e)"),
                               t_bank[g % 2][:], ACT.Copy).then_inc(t_fh, 1)
            for g in range(NC):
                act.wait_ge(t_mv, NC + g + 1)
                act.activation(dev[:, 1, g * BC:(g + 1) * BC], mv[:, 1, g * BC:(g + 1) * BC, 1], ACT.Sqrt,
                               bias=eps[:]).then_inc(t_dev, 1)
            for g in range(NC):
                act.wait_ge(t_y, NC + g + 1)
                act.dma_start(out[g * CW:(g + 1) * CW, :].rearrange("(b p) e -> p b e", p=BT),
                              z[:, g * BC:(g + 1) * BC, :]).then_inc(stored, 16)

        @block.tensor
        def _(pe):
            pe.wait_ge(w_loaded, 16 * 5)
            pe.matmul(misc[:, 0:E], wk_sb[:], q2l_sb[:], start=True, stop=True)
            pe.matmul(misc[:, E:2 * E], wv_sb[:], vup_sb[:], start=True, stop=True).then_inc(folded, 1)
            pe.wait_ge(x_loaded, 16)
            for n in range(3 * NC):
                if n == 1:
                    pe.wait_ge(folded_sb, 1)
                if n >= 7:
                    pe.wait_ge(evacuated, n - 6)
                if n < 2 * NC:
                    c = n // 2
                    w = wkh_sb if n % 2 else wqT_sb
                    mm = pe.matmul(banks[n % 7][:], w[:], xT_sb[:, c * CW:(c + 1) * CW], start=True, stop=True)
                else:
                    c = n - 2 * NC
                    for b in range(BC):
                        t = c * CW + b * BT
                        mm = pe.matmul(banks[n % 7][:, b * BT:(b + 1) * BT], xT_sb[:, t:t + BT], wvh_sb[:],
                                       start=True, stop=True)
                mm.then_inc(projected, 1)

            def max_tile(b, u, first=False):
                i, c, w = S_TILES[u]
                diagonal = c == i // BC
                bank = s_bank[(b * NS + u) % S_RING]
                if u >= S_RING:
                    pe.wait_ge(s_reduced[b], u - S_RING + 1)
                elif not first:
                    pe.wait_ge(s_reduced[(b + 2) % UNROLL], NS + u - S_RING + 1)
                mm = pe.matmul(bank[:, 0:w], q_aug[0:PAD, b, i * BT:(i + 1) * BT],
                               k_aug[0:PAD, b, c * CW:c * CW + w], start=True, stop=not diagonal)
                if diagonal:
                    mm = pe.matmul(bank[:, w - BT:w], ident_b[:], mask[:], start=False, stop=True)
                mm.then_inc(s_ready[b], 1)

            def score_tile(b, n, k, first=False):
                j, c, o, col = TILES[n][k]
                u = FIRST[n] + k
                if u >= T_RING:
                    pe.wait_ge(t_exped[b], u - T_RING + 1)
                elif not first:
                    pe.wait_ge(t_exped[(b + 2) % UNROLL], NT + u - T_RING + 1)
                pe.matmul(t_bank[(b * NT + u) % T_RING][:, o:CW], k_aug[:, b, j * BT:(j + 1) * BT],
                          q_aug[:, b, c * CW + o:(c + 1) * CW], start=True, stop=True).then_inc(t_ready[b], 1)

            def score_group(b, n, max_tiles, first=False):
                for k in range(len(TILES[n])):
                    score_tile(b, n, k, first)
                    if max_tiles:
                        max_tile(*max_tiles.pop(0))

            def value_group(b, n, first=False):
                if n == 0 and not first:
                    pe.wait_ge(o_copied[(b + 2) % UNROLL], 1)
                pe.wait_ge(t_exped[b], FIRST[n + 1])
                for m, j in enumerate(GROUPS[n]):
                    pe.wait_ge(masked[b], j + 1)
                    c0 = j // BC
                    cols = probs[:, (b * NG + n) % P_RING, m * (NC - c0) * CW:(m + 1) * (NC - c0) * CW]
                    cols = cols.rearrange("p (c q t) -> p c q t", q=BC, t=BT)
                    sums = o_bank[:].rearrange("p (c t) -> p c t", t=BT)
                    for q in range(BC):
                        lo = c0 if BC * c0 + q >= j else c0 + 1
                        if lo < NC:
                            mm = pe.matmul(sums[q * VW:(q + 1) * VW, lo:NC, :], v_head[:, b, j, :],
                                           cols[:, lo - c0:, q, :], start=j == 0, stop=LAST_KEYS[q, lo] == j)
                mm.then_inc(p_used[b], 1)

            LAST_KEYS = {(q, NC - 1): BC * (NC - 1) + q for q in range(BC)}
            LAST_KEYS.update({(q, c): None for q in range(BC) for c in range(NC - 1)})

            def turn_sums(b):
                pe.wait_ge(o_copied[b], 1)
                for c in range(NC):
                    mm = pe.matmul(turned[:, c * BC:(c + 1) * BC, :].rearrange("p b d -> p (b d)"),
                                   ctx_sb[:, c * BT:(c + 1) * BT], sel[:].rearrange("p b d -> p (b d)"),
                                   start=True, stop=True)
                mm.then_inc(ctx_turned[b], 1)

            def turn_max(b):
                pe.wait_ge(max_split[b], 4)
                pe.transpose(max_t, max_parts[:].rearrange("p a b -> p (a b)"), ident_b[:]).then_inc(max_turned[b], 1)

            pe.wait_ge(evacuated, 3 * NC)
            pe.wait_ge(qk_loaded[0], QK_LOADS)
            for u in range(NS):
                max_tile(0, u, first=True)
            pe.wait_ge(qk_loaded[1], QK_LOADS)
            early = [(1, u) for u in range(EARLY)]
            for _ in range(6):
                max_tile(*early.pop(0))
            turn_max(0)
            while len(early) > 8:
                max_tile(*early.pop(0))
            pe.wait_ge(max_loaded[0], MAX_LOADS)
            score_group(0, 0, early, first=True)
            score_group(0, 1, early, first=True)

            def step(b, more, more2, first=False):
                nxt, old = (b + 1) % UNROLL, (b + 2) % UNROLL
                tiles = [(nxt, u) for u in range(EARLY, NS)] if more else []
                tiles += [(old, u) for u in range(EARLY)] if more2 else []
                pe.wait_ge(v_ready[b], 1)
                for n in range(NG):
                    if n == 1:
                        pe.wait_ge(normalised[old], 1)
                    value_group(b, n)
                    if n + 2 < NG:
                        if n + 2 == SPLIT_AFTER and more2:
                            pe.wait_ge(cleared[b], 1)
                        if n + 2 == SPLIT_AFTER + 1 and more2:
                            pe.wait_ge(qk_loaded[old], QK_LOADS)
                        score_group(b, n + 2, tiles)
                        if n + 2 == TURN_MAX_AFTER and more:
                            turn_max(nxt)
                    elif more:
                        if n + 2 == NG:
                            pe.wait_ge(max_loaded[nxt], MAX_LOADS)
                        score_group(nxt, n + 2 - NG, tiles)
                assert not tiles
                if more:
                    pe.wait_ge(max_copied[nxt], 1)
                turn_sums(b)

            with pe.Fori(0, LOOPS) as it:
                for k in range(UNROLL):
                    step(k, True, True)
            for h in range(LOOPS * UNROLL, H):
                step(h % UNROLL, h + 1 < H, h + 2 < H)

            for g in range(NC):
                pe.wait_ge(normalised[(H - 1) % UNROLL], 1)
                if g >= 2:
                    pe.wait_ge(t_hsb, g - 1)
                for b in range(BC):
                    mm = pe.transpose(s_bank[g % 2][:, b * BT:(b + 1) * BT], heads[:, g * BC + b, :], ident_f[:])
                mm.then_inc(t_h, 1)
                pe.wait_ge(t_hsb, g + 1)
                if g >= 2:
                    pe.wait_ge(t_z, g - 1)
                if g == 0:
                    pe.wait_ge(tail_loaded, 64)
                for b in range(BC):
                    mm = pe.matmul(t_bank[g % 2][:, b * BT:(b + 1) * BT], heads_t[:, g % 2, b * BT:(b + 1) * BT],
                                   wout_sb[:], start=True, stop=True)
                mm.then_inc(t_attn, 1)
            pe.wait_ge(t_w, 11)
            for g in range(NC):
                pe.wait_ge(t_yb, g + 1)
                if g >= 2:
                    pe.wait_ge(t_ytsb, g - 1)
                for b in range(BC):
                    mm = pe.transpose(s_bank[g % 2][:, b * BT // 2:(b + 1) * BT // 2].bitcast(bf16),
                                      y_b[:, g * BC + b, :], ident_b[:])
                mm.then_inc(t_yt, 1)
                pe.wait_ge(t_ytsb, g + 1)
                if g < 2:
                    pe.wait_ge(t_z, NC)
                else:
                    pe.wait_ge(t_fh, g - 1)
                for b in range(BC):
                    mm = pe.matmul(t_bank[g % 2][:, b * BT:(b + 1) * BT], y_t[:, g % 2, b * BT:(b + 1) * BT],
                                   w_q[:], start=True, stop=True)
                mm.then_inc(t_f, 1)

        @block.vector
        def _(dve):
            last = UNROLL - 1
            dve.memset(tile_max[:], -3.0e38).then_inc(p_used[last], NG)
            dve.memset(rstd[:, 0, :], 0.0).then_inc(o_copied[last], 1)
            dve.memset(recip[:], 0.0).then_inc(normalised[last], 1)
            dve.wait_ge(constants, 2)
            dve.tensor_copy(sel[:], ident_f[:].rearrange("p (q r) -> p q r", q=BC)[:, :, 0:D + 1]).then_inc(t_w, 1)
            dve.wait_ge(folded, 1)
            dve.tensor_copy(wkh_sb[:], misc[:, 0:E]).then_inc(t_w, 1)
            dve.wait_ge(t_w, 2)
            dve.tensor_copy(wvh_sb[:], misc[:, E:2 * E]).then_inc(folded_sb, 1)
            for n in range(2 * NC):
                c = n // 2
                parts = k_parts if n % 2 else q_parts
                cs = slice(c * CW, (c + 1) * CW)
                dve.wait_ge(evacuated, n + 1)
                dve.tensor_tensor(rest[:, n % 2, :], full[:, n % 2, :], parts[:, 0, cs],
                                  ALU.subtract).then_inc(rest_done, 1)
                dve.wait_ge(rest_done, n + 1)
                dve.tensor_copy(parts[:, 1, cs], rest[:, n % 2, :]).then_inc(part2, 1)
                dve.wait_ge(part2, n + 1)
                dve.tensor_tensor(parts[:, 2, cs], rest[:, n % 2, :], parts[:, 1, cs],
                                  ALU.subtract).then_inc(part3, 1)

            def reduce_tile(b, u):
                i, c, w = S_TILES[u]
                dve.wait_ge(s_ready[b], u + 1)
                dve.tensor_reduce(tile_max[:, b, i, c:c + 1], s_bank[(b * NS + u) % S_RING][:, 0:w], AX.X,
                                  ALU.max).then_inc(s_reduced[b], 1)

            def negate_max(b):
                dve.wait_ge(s_reduced[b], NS)
                dve.tensor_reduce(neg_max[:], tile_max[:, b], AX.X, ALU.max, negate=True).then_inc(max_ready[b], 1)

            def copy_max(b, first=False):
                if not first:
                    dve.wait_ge(max_loaded[(b + 2) % UNROLL], MAX_LOADS)
                dve.wait_ge(max_turned[b], 1)
                dve.tensor_copy(max_rows[:], max_t).then_inc(max_copied[b], 1)

            def normalise(h, b):
                dve.wait_ge(ctx_turned[b], 1)
                dve.reciprocal(recip[:], turned[:, :, D]).then_inc(recip_ready, 1)
                dve.wait_ge(recip_ready, 1)
                dve.sem_clear(recip_ready)
                dve.tensor_tensor(heads[:, :, bass.ds(h * D, D)], turned[:, :, 0:D],
                                  recip[:].rearrange("p (b o) -> p b o", o=1).broadcast_to([BT, NB, D]),
                                  ALU.mult).then_inc(normalised[b], 1)

            COPY_AT = 5
            for u in range(NS):
                reduce_tile(0, u)
            negate_max(0)
            for u in range(EARLY):
                if u == COPY_AT:
                    copy_max(0, first=True)
                reduce_tile(1, u)

            def step(h, b, more, more2):
                nxt, old = (b + 1) % UNROLL, (b + 2) % UNROLL
                if more:
                    for u in range(EARLY, NS):
                        reduce_tile(nxt, u)
                    negate_max(nxt)
                if more2:
                    for u in range(COPY_AT):
                        reduce_tile(old, u)
                if more:
                    copy_max(nxt)
                if more2:
                    for u in range(COPY_AT, EARLY):
                        reduce_tile(old, u)
                normalise(h, b)

            with dve.Fori(0, LOOPS) as it:
                for k in range(UNROLL):
                    step(it * UNROLL + k, k, True, True)
            for h in range(LOOPS * UNROLL, H):
                step(h, h % UNROLL, h + 1 < H, h + 2 < H)

            t_done = [2]

            def w_step(ins):
                ins.then_inc(t_w, 1)
                t_done[0] += 1
                dve.wait_ge(t_w, t_done[0])

            dve.wait_ge(tail_loaded, 64)
            w_step(dve.tensor_scalar(w_t[:, 0, :], wf_sb[:], 448.0, -448.0, ALU.min, ALU.max))
            w_step(dve.tensor_scalar(w_t[:, 1, :], wf_sb[:], 240.0, -240.0, ALU.min, ALU.max))
            w_step(dve.tensor_scalar(w8[:, 0, :], w_t[:, 1, :], 1.0, None, ALU.mult, saturate=False))
            w_step(dve.tensor_scalar(w8[:, 1, :], w_t[:, 0, :], 0.5, None, ALU.mult, saturate=False))
            w_step(dve.tensor_tensor(w_t[:, 2, :], w_t[:, 0, :], w_t[:, 0, :], ALU.mult))
            w_step(dve.tensor_scalar(w_t[:, 2, :], w_t[:, 2, :], 128.0 ** 2, None, ALU.is_ge))
            w_step(dve.scalar_tensor_tensor(out=w_t[:, 3, :], in0=w8[:, 1, :], scalar=2.0, in1=w8[:, 0, :],
                                            op0=ALU.mult, op1=ALU.subtract))
            w_step(dve.tensor_tensor(w_t[:, 1, :], w_t[:, 3, :], w_t[:, 2, :], ALU.mult))
            dve.tensor_tensor(w_q[:], w_t[:, 1, :], w8[:, 0, :], ALU.add).then_inc(t_w, 1)

            def layernorm(which, g, src, dst):
                base = which * NB + g * BC
                for b in range(g * BC, (g + 1) * BC):
                    dve.bn_stats(stats[:, which, b, :], src[:, b, :]).then_inc(t_stat, 1)
                for b in range(g * BC, (g + 1) * BC):
                    dve.wait_ge(t_stat, which * NB + b + 1)
                    ins = dve.bn_aggr(mv[:, which, b, :], stats[:, which, b, :])
                ins.then_inc(t_mv, 1)

            def normal(which, g, src, dst):
                gs = slice(g * BC, (g + 1) * BC)
                dve.wait_ge(t_dev, which * NC + g + 1)
                dve.reciprocal(rstd[:, which, gs], dev[:, which, gs]).then_inc(t_rstd, 1)
                dve.wait_ge(t_rstd, which * NC + g + 1)
                dve.wait_ge(t_mv, which * NC + g + 1)
                for b in range(g * BC, (g + 1) * BC):
                    ins = dve.tensor_scalar(dst[:, b, :], src[:, b, :], mv[:, which, b, 0:1], rstd[:, which, b:b + 1],
                                            ALU.subtract, ALU.mult)
                ins.then_inc(t_y, 1)

            for g in range(NC):
                gs = slice(g * BC, (g + 1) * BC)
                dve.wait_ge(t_attn, g + 1)
                dve.tensor_tensor(z[:, gs, :].rearrange("p b e -> p (b e)"), t_bank[g % 2][:],
                                  x_sb[:, gs, :].rearrange("p b e -> p (b e)"), ALU.add).then_inc(t_z, 1)
                dve.wait_ge(t_z, g + 1)
                layernorm(0, g, z, y)
            for g in range(NC):
                gs = slice(g * BC, (g + 1) * BC)
                normal(0, g, z, y)
                dve.wait_ge(t_y, g + 1)
                dve.tensor_copy(y8[:, gs, :], y[:, gs, :], saturate=False).then_inc(t_y8, 1)
                dve.wait_ge(t_y8, g + 1)
                dve.tensor_copy(y_b[:, gs, :], y8[:, gs, :]).then_inc(t_yb, 1)
                for b in range(g * BC, (g + 1) * BC):
                    ins = dve.tensor_tensor(y[:, b, :], y[:, b, :], bias_sb[:], ALU.add)
                ins.then_inc(t_y8b, 1)
            for g in range(NC):
                gs = slice(g * BC, (g + 1) * BC)
                dve.wait_ge(t_fh, g + 1)
                dve.wait_ge(t_y8b, g + 1)
                dve.tensor_tensor(y[:, gs, :], y[:, gs, :], f_h[:, gs, :], ALU.add).then_inc(t_z, 1)
                dve.wait_ge(t_z, NC + g + 1)
                layernorm(1, g, y, z)
            for g in range(NC):
                normal(1, g, y, z)


_INS = ["x", "xT", "wqT", "wk_down", "wv_down", "q2lT", "v_upT", "woutT", "ffn_wT", "ffn_bias"]


def kernel(L0_attn_hidden_states, L0_attn_Wq, L0_attn_Wk_down, L0_attn_Wv_down, L0_attn_q_to_latent,
           L0_attn_v_up, L0_attn_Wout, L0_ffn_weight, L0_ffn_bias):
    import numpy as np
    import concourse.bacc as bacc
    from concourse import mybir as _mybir
    from concourse.bass_utils import run_bass_kernel_spmd

    x = np.asarray(L0_attn_hidden_states)[0]
    T, E = x.shape
    H, D, L = L0_attn_q_to_latent.shape
    laid = {
        "x": x,
        "xT": x.T,
        "wqT": np.asarray(L0_attn_Wq).T,
        "wk_down": np.asarray(L0_attn_Wk_down),
        "wv_down": np.asarray(L0_attn_Wv_down),
        "q2lT": np.asarray(L0_attn_q_to_latent).reshape(H * D, L).T,
        "v_upT": np.asarray(L0_attn_v_up).transpose(1, 0, 2).reshape(L, H * D),
        "woutT": np.asarray(L0_attn_Wout).T,
        "ffn_wT": np.asarray(L0_ffn_weight).T,
        "ffn_bias": np.asarray(L0_ffn_bias),
    }
    nc = bacc.Bacc("TRN2", target_bir_lowering=False, num_devices=1)
    arrays, args = {}, []
    for name in _INS:
        a = np.ascontiguousarray(laid[name])
        arrays[f"in_{name}"] = a
        args.append(nc.dram_tensor(f"in_{name}", a.shape, _mybir.dt.from_np(a.dtype), kind="ExternalInput").ap())
    out = nc.dram_tensor("out", (T, E), _mybir.dt.from_np(x.dtype), kind="ExternalOutput").ap()
    postln_block_kernel(nc, *args, out)
    r = run_bass_kernel_spmd(nc, [arrays], core_ids=[0])
    return r.results[0]["out"].reshape(1, T, E)
```

```python
import concourse.bass as bass
from concourse import mybir
from contextlib import ExitStack


def postln_block_kernel(nc, x, xT, wqT, wk_down, wv_down, q2lT, v_upT, woutT, ffn_wT, ffn_bias, out):
    f32, bf16, f16 = mybir.dt.float32, mybir.dt.bfloat16, mybir.dt.float16
    fp8 = mybir.dt.float8e4
    ALU, ACT, AX = mybir.AluOpType, mybir.ActivationFunctionType, mybir.AxisListType

    T, E = x.shape
    L = wk_down.shape[0]
    H = 16
    D = E // H
    BT = 128
    NB = T // BT
    CW = 512
    NC = T // CW
    BC = CW // BT
    PARTS = 3
    ROWS = PARTS * PARTS * D
    PAD = 96
    AUG = 128
    BELOW = ROWS // 32 * 32
    VW = 32
    HW = D + 1
    SCALE = 1.0 / 8.0
    EPS = 1e-5
    assert L == 64 and ROWS == 72

    S_TILES = [(i, c, min(CW, (i + 1) * BT - c * CW)) for i in range(NB) for c in range(i // BC + 1)]
    NS = len(S_TILES)
    DIAGONALS = [u for u, (i, c, w) in enumerate(S_TILES) if c == i // BC]
    GROUPS = [[j] for j in range(2 * BC)] + [[8, 9], [10, 11], [12, 13, 14, 15]]
    NG = len(GROUPS)

    def tiles_of(js):
        out = []
        for n, j in enumerate(js):
            c0 = j // BC
            for c in range(c0, NC):
                o = (j - BC * c0) * BT if c == c0 else 0
                out.append((j, c, o, (n * (NC - c0) + c - c0) * CW))
        return out

    TILES = [tiles_of(js) for js in GROUPS]
    FIRST = [sum(len(t) for t in TILES[:n]) for n in range(NG + 1)]
    NT = FIRST[NG]
    LAST_TILES, LAST_ENDS = [], []
    for c in range(NC):
        for j0 in range(0, BC * (c + 1), BC):
            LAST_TILES.append([(j, c, max(j - BC * c, 0) * BT, (j - j0) * CW) for j in range(j0, j0 + BC)])
        LAST_ENDS.append(len(LAST_TILES))
    LAST_NG = len(LAST_TILES)
    LAST_FIRST = [BC * n for n in range(LAST_NG + 1)]

    def layout(last):
        return (LAST_TILES, LAST_FIRST) if last else (TILES, FIRST)

    UNROLL = 3
    S_RING, T_RING, P_RING = 3, 3, 3
    EARLY = 19
    assert NS == NT and H % UNROLL == 1 and sorted(sum(GROUPS, [])) == list(range(NB))

    with ExitStack() as ctx:
        def sb(name, shape, dt=f32):
            return ctx.enter_context(nc.sbuf_tensor(name, shape, dt))

        def sem(name):
            return ctx.enter_context(nc.semaphore(name))

        x_sb = sb("x_sb", [BT, NB, E])
        xT_sb = sb("xT_sb", [E, T])
        wqT_sb = sb("wqT_sb", [E, E])
        wk_sb = sb("wk_sb", [L, E])
        wv_sb = sb("wv_sb", [L, E])
        q2l_sb = sb("q2l_sb", [L, E])
        vup_sb = sb("vup_sb", [L, E])
        wout_sb = sb("wout_sb", [E, E])
        wf_sb = sb("wf_sb", [E, E])
        bias_sb = sb("bias_sb", [BT, E])
        wkh_sb = sb("wkh_sb", [E, E])
        wvh_sb = sb("wvh_sb", [E, E])
        rest = sb("rest", [E, 2, CW])
        q_parts = sb("q_parts", [E, PARTS, T], bf16)
        k_parts = sb("k_parts", [E, PARTS, T], bf16)
        q_aug = sb("q_aug", [AUG, UNROLL, T], bf16)
        k_aug = sb("k_aug", [AUG, UNROLL, T], bf16)
        v_all = sb("v_all", [BT, NB, E])
        v_head = sb("v_head", [BT, UNROLL, NB, VW])
        probs = sb("probs", [BT, P_RING, T])
        ctx_sb = sb("ctx_sb", [BT, CW])
        heads = sb("heads", [BT, NB, E])
        tile_max = sb("tile_max", [BT, UNROLL, NB, BC])
        neg_max = sb("neg_max", [BT, NB])
        max_rest = sb("max_rest", [BT, NB])
        max_parts = sb("max_parts", [BT, PARTS, NB], bf16)
        max_rows = sb("max_rows", [PARTS * NB, BT], bf16)
        recip = sb("recip", [BT, NB, UNROLL])
        sel = sb("sel", [BT, BC, UNROLL * HW])
        ident_f = sb("ident_f", [BT, BT])
        ident_b = sb("ident_b", [BT, BT], bf16)
        mask = sb("mask", [BT, CW])
        masked_scores = sb("masked_scores", [BT, BC, CW])
        w8 = sb("w8", [E, 2, E], fp8)
        w_t = sb("w_t", [E, 4, E])
        w_q = sb("w_q", [E, E], bf16)
        heads_t = sb("heads_t", [E, NC, CW])
        z = sb("z", [BT, NB, E])
        y = sb("y", [BT, NB, E])
        y8 = sb("y8", [BT, NB, E], fp8)
        y_b = sb("y_b", [BT, NB, E], bf16)
        y_t = sb("y_t", [E, NC, CW], bf16)
        f_h = sb("f_h", [BT, NB, E], f16)
        stats = sb("stats", [BT, 2, NB, 6])
        mv = sb("mv", [BT, 2, NB, 2])
        dev = sb("dev", [BT, 2, NB])
        rstd = sb("rstd", [BT, 2, NB])
        shift = sb("shift", [BT, 2, NB])
        eps = sb("eps", [BT, 1])

        s_bank = [ctx.enter_context(nc.psum_tensor(f"s_bank{n}", [BT, CW], f32)) for n in range(S_RING)]
        t_bank = [ctx.enter_context(nc.psum_tensor(f"t_bank{n}", [BT, CW], f32)) for n in range(T_RING)]
        o_bank = ctx.enter_context(nc.psum_tensor("o_bank", [BT, CW], f32))
        misc = ctx.enter_context(nc.psum_tensor("misc", [BT, CW], f32))
        turned = misc[:, 0:NB * UNROLL * HW].rearrange("p (b r) -> p b r", r=UNROLL * HW)
        max_t = misc[0:PARTS * NB, CW - BT // 2:].bitcast(bf16)

        q_dram = nc.dram_tensor("q_parts_dram", [E, PARTS, T], bf16, kind="Internal").ap()
        k_dram = nc.dram_tensor("k_parts_dram", [E, PARTS, T], bf16, kind="Internal").ap()

        k_weights_loaded = sem("k_weights_loaded")
        q_weights_loaded = sem("q_weights_loaded")
        v_weights_loaded = sem("v_weights_loaded")
        xT_loaded = [sem(f"xT_loaded{c}") for c in range(NC)]
        tail_loaded = sem("tail_loaded")
        constants = sem("constants")
        preset = sem("preset")
        k_folded = sem("k_folded")
        v_folded = sem("v_folded")
        k_folded_sb = sem("k_folded_sb")
        v_folded_sb = sem("v_folded_sb")
        projected = sem("projected")
        first_part = sem("first_part")
        rest_ready = sem("rest_ready")
        second_part = sem("second_part")
        third_part = sem("third_part")
        values_copied = sem("values_copied")
        q_stored = [sem(f"q_stored{c}") for c in range(NC)]
        k_stored = [sem(f"k_stored{c}") for c in range(NC)]
        chunk_loaded = [sem(f"chunk_loaded{c}") for c in range(NC)]

        def head_sems(name):
            return [sem(f"{name}{b}") for b in range(UNROLL)]

        qk_loaded = head_sems("qk_loaded")
        max_loaded = head_sems("max_loaded")
        s_ready = head_sems("s_ready")
        s_reduced = head_sems("s_reduced")
        max_ready = head_sems("max_ready")
        max_split = head_sems("max_split")
        max_turned = head_sems("max_turned")
        max_copied = head_sems("max_copied")
        t_ready = head_sems("t_ready")
        t_exped = head_sems("t_exped")
        masked = head_sems("masked")
        v_ready = head_sems("v_ready")
        p_used = head_sems("p_used")
        o_copied = head_sems("o_copied")
        ctx_turned = head_sems("ctx_turned")
        normalised = head_sems("normalised")
        cleared = head_sems("cleared")
        HEAD_SEMS = [cleared, qk_loaded, max_loaded, s_ready, s_reduced, max_ready, max_split, max_turned, max_copied,
                     t_ready, t_exped, masked, v_ready, p_used, o_copied, ctx_turned, normalised]
        recip_ready = sem("recip_ready")
        sums_copied = sem("sums_copied")
        sums_turned = sem("sums_turned")
        sums_inverted = sem("sums_inverted")
        heads_ready = sem("heads_ready")
        heads_turned = sem("heads_turned")
        heads_copied = sem("heads_copied")
        attn_ready = sem("attn_ready")
        z_ready = sem("z_ready")
        z_stats = sem("z_stats")
        z_moments = sem("z_moments")
        z_dev = sem("z_dev")
        z_inverted = sem("z_inverted")
        z_shift = sem("z_shift")
        y_ready = sem("y_ready")
        y_rounded = sem("y_rounded")
        yb_ready = sem("yb_ready")
        y_biased = sem("y_biased")
        y_turned = sem("y_turned")
        y_copied = sem("y_copied")
        ffn_ready = sem("ffn_ready")
        ffn_rounded = sem("ffn_rounded")
        r_ready = sem("r_ready")
        r_stats = sem("r_stats")
        r_moments = sem("r_moments")
        r_dev = sem("r_dev")
        r_inverted = sem("r_inverted")
        r_shift = sem("r_shift")
        out_ready = sem("out_ready")
        last_out_ready = sem("last_out_ready")
        weights_ready = sem("weights_ready")
        stored = sem("stored")

        MASK_DONE, ONES_DONE, CONSTANTS = 5, 6, 11 + UNROLL
        PRESETS = 2
        LOOPS = (H - 2) // UNROLL
        QK_LOADS, MAX_LOADS = 16 * (PARTS + 1), 16
        SPLIT_AFTER, TURN_MAX_AFTER = 7, 9
        block = ctx.enter_context(nc.Block())
        banks = t_bank + [o_bank]
        chunk_bank = s_bank + [o_bank]
        LAST = (H - 1) % UNROLL
        WEIGHT_STEPS = 9

        @block.sync
        def _(sp):
            def load_xT(c):
                cs = slice(c * CW, (c + 1) * CW)
                sp.dma_start(xT_sb[:, cs], xT[:, cs]).then_inc(xT_loaded[c], 16)

            sp.dma_start(wqT_sb[:], wqT).then_inc(q_weights_loaded, 16)
            load_xT(0)
            sp.dma_start(wk_sb[:], wk_down).then_inc(k_weights_loaded, 16)
            sp.dma_start(q2l_sb[:], q2lT).then_inc(k_weights_loaded, 16)
            for c in range(1, NC):
                load_xT(c)
            sp.dma_start(wv_sb[:], wv_down).then_inc(v_weights_loaded, 16)
            sp.dma_start(vup_sb[:], v_upT).then_inc(v_weights_loaded, 16)

            def store_parts(n):
                c, is_k = n // 2, n % 2
                cs = slice(c * CW, (c + 1) * CW)
                dst, src, done = (k_dram, k_parts, k_stored) if is_k else (q_dram, q_parts, q_stored)
                sp.wait_ge(third_part, n + 1)
                sp.dma_start(dst[:, :, cs], src[:, :, cs]).then_inc(done[c], 16)

            def load_head(h, b, cs, done):
                width, size = cs.stop - cs.start, PARTS * D
                k_rows = k_dram[bass.ds(h * D, D), :, cs].rearrange("d j t -> (d j) t").rearrange("(o r) t -> o r t", o=1)
                sp.dma_start(k_aug[0:ROWS, b, cs], k_rows.broadcast_to([PARTS, size, width])).then_inc(done, 16)
                for i in range(PARTS):
                    q_rows = q_dram[bass.ds(h * D, D), i:i + 1, cs]
                    sp.dma_start(q_aug[i * size:(i + 1) * size, b, cs],
                                 q_rows.broadcast_to([D, PARTS, width])).then_inc(done, 16)

            def load_chunk(c):
                sp.wait_ge(q_stored[c], 16)
                sp.wait_ge(k_stored[c], 16)
                load_head(0, 0, slice(c * CW, (c + 1) * CW), chunk_loaded[c])

            def load_max(b):
                sp.wait_ge(max_copied[b], 1)
                sp.dma_start(q_aug[PAD:PAD + PARTS, b, :], max_rows[:]).then_inc(max_loaded[b], 16)

            for n in range(4):
                store_parts(n)
            sp.wait_ge(preset, PRESETS)
            sp.wait_ge(constants, ONES_DONE)
            for c in range(NC):
                load_chunk(c)
                if c + 2 < NC:
                    store_parts(2 * c + 4)
                    store_parts(2 * c + 5)
            sp.wait_ge(constants, CONSTANTS)
            load_head(1, 1, slice(0, T), qk_loaded[1])
            load_max(0)

            def step(h, b, more):
                nxt, old = (b + 1) % UNROLL, (b + 2) % UNROLL
                if more:
                    sp.wait_ge(t_exped[b], FIRST[2] + 1)
                    sp.wait_ge(p_used[b], 2)
                    sp.wait_ge(v_ready[nxt], 1)
                    for sems in HEAD_SEMS:
                        sp.sem_clear(sems[old])
                    sp.sem_inc(cleared[b], 1)
                    load_head(h + 2, old, slice(0, T), qk_loaded[old])
                load_max(nxt)

            with sp.Fori(0, LOOPS) as it:
                for k in range(UNROLL):
                    step(it * UNROLL + k, k, True)
            for h in range(LOOPS * UNROLL, H - 1):
                step(h, h % UNROLL, h + 2 < H)
            for c in range(NC):
                cs = slice(c * CW, (c + 1) * CW)
                if c < NC - 1:
                    sp.wait_ge(out_ready, c + 1)
                else:
                    sp.wait_ge(last_out_ready, 1)
                sp.dma_start(out[cs, :].rearrange("(b p) e -> p b e", p=BT),
                             z[:, c * BC:(c + 1) * BC, :]).then_inc(stored, 16)
            sp.wait_ge(stored, 16 * NC)

        @block.gpsimd
        def _(pool):
            pool.memset(ident_f[:], 0.0).then_inc(constants, 1)
            pool.wait_ge(constants, 1)
            pool.affine_select(out=ident_f[:], in_=ident_f[:], compare_op=ALU.not_equal, fill=1.0,
                               base=0, pattern=[[-1, BT]], channel_multiplier=1).then_inc(constants, 1)
            pool.wait_ge(constants, 2)
            pool.tensor_copy(ident_b[:], ident_f[:]).then_inc(constants, 1)
            pool.wait_ge(constants, 3)
            pool.memset(mask[:], 0.0).then_inc(constants, 1)
            pool.wait_ge(constants, 4)
            pool.affine_select(out=mask[:, CW - BT:], in_=mask[:, CW - BT:], compare_op=ALU.is_ge, fill=-1e30,
                               base=0, pattern=[[-1, BT]], channel_multiplier=1).then_inc(constants, 1)
            pool.wait_ge(constants, 5)
            pool.memset(k_aug[PAD:AUG, 0, :], 1.0).then_inc(constants, 1)
            pool.wait_ge(constants, 6)
            pool.memset(eps[:], EPS).then_inc(constants, 1)
            pool.wait_ge(constants, 7)
            pool.memset(q_aug[BELOW:AUG, 1:UNROLL, :].bitcast(f32), 0.0).then_inc(constants, 1)
            pool.wait_ge(constants, 8)
            pool.memset(k_aug[BELOW:PAD, 1:UNROLL, :].bitcast(f32), 0.0).then_inc(constants, 1)
            pool.wait_ge(constants, 9)
            pool.memset(k_aug[PAD:AUG, 1:UNROLL, :], 1.0).then_inc(constants, 1)
            pool.wait_ge(constants, 10)
            pool.memset(v_head[:], 0.0).then_inc(constants, 1)
            pool.wait_ge(constants, 11)
            for b in range(UNROLL):
                pool.memset(v_head[:, b, :, b * HW + D:(b + 1) * HW], 1.0).then_inc(constants, 1)
            pool.wait_ge(constants, 11 + UNROLL)
            pool.wait_ge(chunk_loaded[NC - 1], QK_LOADS)
            pool.dma_start(x_sb[:], x.rearrange("(b p) e -> p b e", p=BT)).then_inc(tail_loaded, 16)
            pool.dma_start(wout_sb[:], woutT).then_inc(tail_loaded, 16)
            pool.dma_start(wf_sb[:], ffn_wT).then_inc(tail_loaded, 16)
            pool.dma_start(bias_sb[:], ffn_bias.rearrange("(o e) -> o e", o=1).broadcast_to([BT, E])).then_inc(
                tail_loaded, 16)

            def copy_values(h, b):
                pool.tensor_copy(v_head[:, b, :, b * HW:b * HW + D], v_all[:, :, bass.ds(h * D, D)]).then_inc(v_ready[b], 1)

            def split_max(b, first=False):
                done = max_split[b]
                pool.wait_ge(max_ready[b], 1)
                if not first:
                    pool.wait_ge(max_turned[(b + 2) % UNROLL], 1)
                pool.tensor_copy(max_parts[:, 0, :], neg_max[:]).then_inc(done, 1)
                pool.wait_ge(done, 1)
                pool.tensor_tensor(max_rest[:], neg_max[:], max_parts[:, 0, :], ALU.subtract).then_inc(done, 1)
                pool.wait_ge(done, 2)
                pool.tensor_copy(max_parts[:, 1, :], max_rest[:]).then_inc(done, 1)
                pool.wait_ge(done, 3)
                pool.tensor_tensor(max_parts[:, 2, :], max_rest[:], max_parts[:, 1, :], ALU.subtract).then_inc(done, 1)

            def mask_group(b, n, last=False):
                tiles, start = layout(last)
                for k, (j, c, o, col) in enumerate(tiles[n]):
                    if c == j // BC:
                        pool.wait_ge(t_exped[b], start[n] + k + 1)
                        d = probs[:, (b * NG + n) % P_RING, col + o:col + o + BT]
                        pool.affine_select(out=d, in_=d, compare_op=ALU.is_ge, fill=0.0, base=0,
                                           pattern=[[1, BT]], channel_multiplier=-1).then_inc(masked[b], 1)

            pool.wait_ge(values_copied, NC)
            copy_values(0, 0)
            split_max(0, first=True)
            mask_group(0, 0)
            mask_group(0, 1)

            def step(h, b, last_next=False):
                nxt, old = (b + 1) % UNROLL, (b + 2) % UNROLL
                pool.wait_ge(p_used[old], NG)
                copy_values(h + 1, nxt)
                for n in range(2, NG):
                    mask_group(b, n)
                    if n == SPLIT_AFTER:
                        split_max(nxt)
                mask_group(nxt, 0, last_next)
                mask_group(nxt, 1, last_next)

            with pool.Fori(0, LOOPS) as it:
                for k in range(UNROLL):
                    step(it * UNROLL + k, k)
            for h in range(LOOPS * UNROLL, H - 1):
                step(h, h % UNROLL, h + 2 == H)
            for n in range(2, LAST_NG):
                mask_group(LAST, n, True)
            for c in range(NC):
                pool.wait_ge(y_ready, c + 1)
                pool.wait_ge(y_rounded, c + 1)
                for t in range(c * BC, (c + 1) * BC):
                    ins = pool.tensor_tensor(y[:, t, :], y[:, t, :], bias_sb[:], ALU.add)
                ins.then_inc(y_biased, 1)

        @block.scalar
        def _(act):
            def part(n, p):
                c = n // 2
                return (k_parts if n % 2 else q_parts)[:, p, c * CW:(c + 1) * CW]

            def take_first(n):
                act.wait_ge(projected, n + 1)
                act.activation(part(n, 0), banks[n % 4][:], ACT.Copy).then_inc(first_part, 1)

            def take_second(n):
                act.wait_ge(rest_ready, n + 1)
                act.activation(part(n, 1), rest[:, n % 2, :], ACT.Copy).then_inc(second_part, 1)

            act.wait_ge(k_folded, 1)
            act.activation(wkh_sb[:], misc[:, 0:E], ACT.Copy, scale=SCALE).then_inc(k_folded_sb, 1)

            take_first(0)
            take_second(0)
            take_first(1)
            take_second(1)
            for n in range(2, 2 * NC):
                take_first(n)
                if n > 2:
                    take_second(n - 1)
            take_second(2 * NC - 1)
            act.wait_ge(v_folded, 1)
            act.activation(wvh_sb[:], misc[:, E:2 * E], ACT.Copy).then_inc(v_folded_sb, 1)
            for c in range(NC):
                act.wait_ge(projected, 2 * NC + c + 1)
                act.activation(v_all[:, c * BC:(c + 1) * BC, :].rearrange("p b e -> p (b e)"),
                               banks[c][:], ACT.Copy).then_inc(values_copied, 1)

            def exp_group(b, n, first=False, last=False):
                if n >= P_RING:
                    act.wait_ge(p_used[b], n - P_RING + 1)
                elif not first:
                    act.wait_ge(p_used[(b + 2) % UNROLL], NG + n - P_RING + 1)
                tiles, start = layout(last)
                for k, (j, c, o, col) in enumerate(tiles[n]):
                    u = start[n] + k
                    act.wait_ge(t_ready[b], u + 1)
                    act.activation(probs[:, (b * NG + n) % P_RING, col + o:col + CW],
                                   t_bank[(b * NT + u) % T_RING][:, o:CW], ACT.Exp).then_inc(t_exped[b], 1)

            def copy_max(b, first=False):
                if not first:
                    act.wait_ge(max_loaded[(b + 2) % UNROLL], MAX_LOADS)
                act.wait_ge(max_turned[b], 1)
                act.activation(max_rows[:], max_t, ACT.Copy).then_inc(max_copied[b], 1)

            def copy_sums(b):
                act.wait_ge(p_used[b], NG)
                act.activation(ctx_sb[:], o_bank[:], ACT.Copy).then_inc(o_copied[b], 1)

            copy_max(0, first=True)
            exp_group(0, 0, first=True)
            exp_group(0, 1, first=True)

            def step(b, last_next=False):
                nxt = (b + 1) % UNROLL
                for n in range(2, NG):
                    exp_group(b, n)
                    if n == TURN_MAX_AFTER:
                        copy_max(nxt)
                exp_group(nxt, 0, last=last_next)
                if b == UNROLL - 1:
                    copy_sums(b)
                exp_group(nxt, 1, last=last_next)

            with act.Fori(0, LOOPS) as it:
                for k in range(UNROLL):
                    step(k)
            for h in range(LOOPS * UNROLL, H - 1):
                step(h % UNROLL, h + 2 == H)
            for n in range(1, LAST_NG):
                if n >= 2:
                    exp_group(LAST, n, last=True)
                if n in LAST_ENDS:
                    c = LAST_ENDS.index(n)
                    act.wait_ge(p_used[LAST], n)
                    act.activation(ctx_sb[:, c * BT:(c + 1) * BT], chunk_bank[c][:, 0:BT],
                                   ACT.Copy).then_inc(sums_copied, 1)

            def deviation(c, which, moments, done):
                cs = slice(c * BC, (c + 1) * BC)
                act.wait_ge(moments, c + 1)
                act.activation(dev[:, which, cs], mv[:, which, cs, 1], ACT.Sqrt, bias=eps[:]).then_inc(done, 1)

            def first_deviation(c):
                deviation(c, 0, z_moments, z_dev)

            def second_deviation(c):
                deviation(c, 1, r_moments, r_dev)

            def copy_heads(c):
                act.wait_ge(heads_turned, c + 1)
                act.activation(heads_t[:, c, :], chunk_bank[c][:], ACT.Copy).then_inc(heads_copied, 1)

            def copy_y(c):
                act.wait_ge(y_turned, c + 1)
                act.activation(y_t[:, c, :], chunk_bank[c][:, 0:CW // 2].bitcast(bf16), ACT.Copy).then_inc(y_copied, 1)

            def round_ffn(c):
                act.wait_ge(ffn_ready, c + 1)
                act.activation(f_h[:, c * BC:(c + 1) * BC, :].rearrange("p b e -> p (b e)"), chunk_bank[c][:],
                               ACT.Copy).then_inc(ffn_rounded, 1)

            def norm(c, which, src, dst, inverted, shifted, done):
                act.wait_ge(inverted, c + 1)
                act.wait_ge(shifted, c + 1)
                for t in range(c * BC, (c + 1) * BC):
                    ins = act.activation(dst[:, t, :], src[:, t, :], ACT.Identity, bias=shift[:, which, t:t + 1],
                                         scale=rstd[:, which, t:t + 1])
                ins.then_inc(done, 1)

            def first_norm(c):
                norm(c, 0, z, y, z_inverted, z_shift, y_ready)

            def second_norm(c):
                norm(c, 1, y, z, r_inverted, r_shift, out_ready)

            def widen_y(c):
                act.wait_ge(y_rounded, c + 1)
                act.activation(y_b[:, c * BC:(c + 1) * BC, :], y8[:, c * BC:(c + 1) * BC, :],
                               ACT.Copy).then_inc(yb_ready, 1)

            first_deviation(0)
            first_deviation(1)
            first_norm(0)
            copy_heads(3)
            first_norm(1)
            first_deviation(2)
            widen_y(0)
            widen_y(1)
            copy_y(0)
            first_norm(2)
            copy_y(1)
            round_ffn(0)
            first_deviation(3)
            widen_y(2)
            round_ffn(1)
            copy_y(2)
            first_norm(3)
            second_deviation(0)
            round_ffn(2)
            widen_y(3)
            copy_y(3)
            second_deviation(1)
            second_norm(0)
            round_ffn(3)
            second_deviation(2)
            second_norm(1)
            second_deviation(3)
            second_norm(2)

        @block.tensor
        def _(pe):
            pe.wait_ge(q_weights_loaded, 16)
            for n in range(2 * NC):
                c, is_k = n // 2, n % 2
                if n == 1:
                    pe.wait_ge(k_weights_loaded, 32)
                    pe.matmul(misc[:, 0:E], wk_sb[:], q2l_sb[:], start=True, stop=True).then_inc(k_folded, 1)
                    pe.wait_ge(k_folded_sb, 1)
                if not is_k:
                    pe.wait_ge(xT_loaded[c], 16)
                if n >= 4:
                    pe.wait_ge(rest_ready, n - 3)
                pe.matmul(banks[n % 4][:], (wkh_sb if is_k else wqT_sb)[:], xT_sb[:, c * CW:(c + 1) * CW],
                          start=True, stop=True).then_inc(projected, 1)
            pe.wait_ge(v_weights_loaded, 32)
            pe.matmul(misc[:, E:2 * E], wv_sb[:], vup_sb[:], start=True, stop=True).then_inc(v_folded, 1)

            def project_values(i):
                c, t = i // BC, i * BT
                if i == 0:
                    pe.wait_ge(v_folded_sb, 1)
                pe.wait_ge(rest_ready, NC + c + 1)
                mm = pe.matmul(banks[c][:, t - c * CW:t - c * CW + BT], xT_sb[:, t:t + BT], wvh_sb[:],
                               start=True, stop=True)
                if i % BC == BC - 1:
                    mm.then_inc(projected, 1)

            def max_tile(b, u, first=False):
                i, c, w = S_TILES[u]
                bank = s_bank[(b * NS + u) % S_RING]
                if u >= S_RING:
                    pe.wait_ge(s_reduced[b], u - S_RING + 1)
                elif not first:
                    pe.wait_ge(s_reduced[(b + 2) % UNROLL], NS + u - S_RING + 1)
                pe.matmul(bank[:, 0:w], q_aug[0:PAD, b, i * BT:(i + 1) * BT],
                          k_aug[0:PAD, b, c * CW:c * CW + w], start=True, stop=True).then_inc(s_ready[b], 1)

            def score_tile(b, n, k, first=False, last=False):
                tiles, start = layout(last)
                j, c, o, col = tiles[n][k]
                u = start[n] + k
                if u >= T_RING:
                    pe.wait_ge(t_exped[b], u - T_RING + 1)
                elif not first:
                    pe.wait_ge(t_exped[(b + 2) % UNROLL], NT + u - T_RING + 1)
                pe.matmul(t_bank[(b * NT + u) % T_RING][:, o:CW], k_aug[:, b, j * BT:(j + 1) * BT],
                          q_aug[:, b, c * CW + o:(c + 1) * CW], start=True, stop=True).then_inc(t_ready[b], 1)

            def score_group(b, n, max_tiles, first=False, last=False):
                for k in range(len(layout(last)[0][n])):
                    score_tile(b, n, k, first, last)
                    if max_tiles:
                        max_tile(*max_tiles.pop(0))

            def value_group(b, n):
                if n == 0 and b == 0:
                    pe.wait_ge(o_copied[UNROLL - 1], 1)
                pe.wait_ge(t_exped[b], FIRST[n + 1])
                for m, j in enumerate(GROUPS[n]):
                    pe.wait_ge(masked[b], j + 1)
                    c0 = j // BC
                    cols = probs[:, (b * NG + n) % P_RING, m * (NC - c0) * CW:(m + 1) * (NC - c0) * CW]
                    cols = cols.rearrange("p (c q t) -> p c q t", q=BC, t=BT)
                    sums = o_bank[:].rearrange("p (c t) -> p c t", t=BT)
                    for q in range(BC):
                        lo = c0 if BC * c0 + q >= j else c0 + 1
                        if lo < NC:
                            mm = pe.matmul(sums[q * VW:(q + 1) * VW, lo:NC, :], v_head[:, b, j, :],
                                           cols[:, lo - c0:, q, :], start=j == 0 and b == 0,
                                           stop=lo == NC - 1 and BC * lo + q == j and b == UNROLL - 1)
                mm.then_inc(p_used[b], 1)

            def turn_sums(b):
                pe.wait_ge(o_copied[b], 1)
                for c in range(NC):
                    mm = pe.matmul(turned[:, c * BC:(c + 1) * BC, :].rearrange("p b r -> p (b r)"),
                                   ctx_sb[:, c * BT:(c + 1) * BT], sel[:].rearrange("p b r -> p (b r)"),
                                   start=True, stop=True)
                mm.then_inc(ctx_turned[b], 1)

            def turn_max(b):
                pe.wait_ge(max_split[b], 4)
                pe.transpose(max_t, max_parts[:].rearrange("p a b -> p (a b)"), ident_b[:]).then_inc(max_turned[b], 1)

            for u, (i, c, w) in enumerate(S_TILES):
                if i % BC == 0 and c == 0:
                    pe.wait_ge(chunk_loaded[i // BC], QK_LOADS)
                max_tile(0, u, first=True)
                if c == i // BC:
                    project_values(i)
            pe.wait_ge(qk_loaded[1], QK_LOADS)
            early = [(1, u) for u in range(EARLY)]
            for _ in range(6):
                max_tile(*early.pop(0))
            turn_max(0)
            while len(early) > 8:
                max_tile(*early.pop(0))
            pe.wait_ge(values_copied, NC)
            pe.wait_ge(max_loaded[0], MAX_LOADS)
            score_group(0, 0, early, first=True)
            score_group(0, 1, early, first=True)

            def step(b, more2):
                nxt, old = (b + 1) % UNROLL, (b + 2) % UNROLL
                tiles = [(nxt, u) for u in range(EARLY, NS)]
                tiles += [(old, u) for u in range(EARLY)] if more2 else []
                pe.wait_ge(v_ready[b], 1)
                for n in range(NG):
                    if n == 1 and b == 0:
                        pe.wait_ge(normalised[old], 1)
                    value_group(b, n)
                    if n + 2 < NG:
                        if n + 2 == SPLIT_AFTER and more2:
                            pe.wait_ge(cleared[b], 1)
                        if n + 2 == SPLIT_AFTER + 1 and more2:
                            pe.wait_ge(qk_loaded[old], QK_LOADS)
                        score_group(b, n + 2, tiles)
                        if n + 2 == TURN_MAX_AFTER:
                            turn_max(nxt)
                    else:
                        if n + 2 == NG:
                            pe.wait_ge(max_loaded[nxt], MAX_LOADS)
                        score_group(nxt, n + 2 - NG, tiles, last=not more2)
                assert not tiles
                if b == UNROLL - 1:
                    pe.wait_ge(max_copied[nxt], 1)
                    turn_sums(b)

            with pe.Fori(0, LOOPS) as it:
                for k in range(UNROLL):
                    step(k, True)
            for h in range(LOOPS * UNROLL, H - 1):
                step(h % UNROLL, h + 2 < H)

            def last_value_part(n, part):
                if part == 0:
                    pe.wait_ge(t_exped[LAST], LAST_FIRST[n + 1])
                half = len(LAST_TILES[n]) // 2
                for j, c, o, col in LAST_TILES[n][part * half:(part + 1) * half]:
                    if c == j // BC:
                        pe.wait_ge(masked[LAST], j + 1)
                    for q in range(o // BT, BC):
                        p0 = col + q * BT
                        mm = pe.matmul(chunk_bank[c][q * VW:(q + 1) * VW, 0:BT], v_head[:, LAST, j, :],
                                       probs[:, (LAST * NG + n) % P_RING, p0:p0 + BT],
                                       start=j == 0, stop=j == BC * c + q)
                if part == 1:
                    mm.then_inc(p_used[LAST], 1)

            def turn_last_sums(c):
                pe.wait_ge(sums_copied, c + 1)
                pe.matmul(chunk_bank[c][:, 0:BC * HW].rearrange("p (b r) -> p b r", r=HW),
                          ctx_sb[:, c * BT:(c + 1) * BT], sel[:, :, 0:HW], start=True, stop=True).then_inc(sums_turned, 1)

            def turn_heads(c):
                pe.wait_ge(heads_ready, c + 1)
                for b in range(BC):
                    mm = pe.transpose(chunk_bank[c][:, b * BT:(b + 1) * BT], heads[:, c * BC + b, :], ident_f[:])
                mm.then_inc(heads_turned, 1)

            def project_out(c, blocks=range(BC)):
                pe.wait_ge(heads_copied, c + 1)
                for b in blocks:
                    mm = pe.matmul(chunk_bank[c][:, b * BT:(b + 1) * BT], heads_t[:, c, b * BT:(b + 1) * BT],
                                   wout_sb[:], start=True, stop=True)
                if b == BC - 1:
                    mm.then_inc(attn_ready, 1)

            def turn_y(c):
                pe.wait_ge(yb_ready, c + 1)
                for b in range(BC):
                    mm = pe.transpose(chunk_bank[c][:, b * BT // 2:(b + 1) * BT // 2].bitcast(bf16),
                                      y_b[:, c * BC + b, :], ident_b[:])
                mm.then_inc(y_turned, 1)

            def linear(c):
                pe.wait_ge(y_copied, c + 1)
                for b in range(BC):
                    mm = pe.matmul(chunk_bank[c][:, b * BT:(b + 1) * BT], y_t[:, c, b * BT:(b + 1) * BT],
                                   w_q[:], start=True, stop=True)
                mm.then_inc(ffn_ready, 1)

            pe.wait_ge(tail_loaded, 64)
            pe.wait_ge(v_ready[LAST], 1)
            for n in range(LAST_NG):
                last_value_part(n, 0)
                for k in range(BC):
                    if k == BC // 2:
                        last_value_part(n, 1)
                    if n + 2 < LAST_NG:
                        score_tile(LAST, n + 2, k, last=True)
                    for c, end in enumerate(LAST_ENDS[:-1]):
                        if n == end and k == 1:
                            turn_last_sums(c)
                        if n == end + 1 and k == 1:
                            turn_heads(c)
                        if n == end + 2 and k % 2 and c < 2:
                            project_out(c, range(k - 1, k + 1))
            project_out(2)
            turn_last_sums(3)
            turn_heads(3)
            project_out(3)
            pe.wait_ge(weights_ready, WEIGHT_STEPS)
            turn_y(0)
            turn_y(1)
            linear(0)
            linear(1)
            turn_y(2)
            linear(2)
            turn_y(3)
            linear(3)

        @block.vector
        def _(dve):
            last = UNROLL - 1
            dve.memset(tile_max[:], -3.0e38).then_inc(p_used[last], NG)
            dve.memset(rstd[:, 0, :], 0.0).then_inc(o_copied[last], 1)
            dve.memset(recip[:], 0.0).then_inc(normalised[last], 1)
            dve.memset(q_aug[BELOW:AUG, 0, :].bitcast(f32), 0.0).then_inc(preset, 1)
            dve.memset(k_aug[BELOW:PAD, 0, :].bitcast(f32), 0.0).then_inc(preset, 1)
            dve.wait_ge(constants, 2)
            dve.tensor_copy(sel[:], ident_f[:].rearrange("p (q r) -> p q r", q=BC)[:, :, 0:UNROLL * HW]).then_inc(preset, 1)

            def part(n, p):
                c = n // 2
                return (k_parts if n % 2 else q_parts)[:, p, c * CW:(c + 1) * CW]

            def subtract_first(n):
                dve.wait_ge(first_part, n + 1)
                if n >= 2:
                    dve.wait_ge(third_part, n - 1)
                dve.tensor_tensor(rest[:, n % 2, :], banks[n % 4][:], part(n, 0), ALU.subtract).then_inc(rest_ready, 1)

            def subtract_second(n):
                dve.wait_ge(second_part, n + 1)
                dve.tensor_tensor(part(n, 2), rest[:, n % 2, :], part(n, 1), ALU.subtract).then_inc(third_part, 1)

            for n in range(2):
                subtract_first(n)
                subtract_second(n)
            for n in range(2, 2 * NC):
                subtract_first(n)
                if n > 2:
                    subtract_second(n - 1)
            subtract_second(2 * NC - 1)

            def reduce_tile(b, u):
                i, c, w = S_TILES[u]
                dve.wait_ge(s_ready[b], u + 1)
                scores, top = s_bank[(b * NS + u) % S_RING][:, 0:w], tile_max[:, b, i, c:c + 1]
                if c == i // BC:
                    if i >= BC:
                        dve.wait_ge(s_reduced[b], DIAGONALS[i - BC] + 1)
                    ins = dve.tensor_tensor_reduce(masked_scores[:, i % BC, 0:w], scores, mask[:, CW - w:], 1.0, -3.0e38,
                                                   ALU.add, ALU.max, top)
                else:
                    ins = dve.tensor_reduce(top, scores, AX.X, ALU.max)
                ins.then_inc(s_reduced[b], 1)

            def negate_max(b):
                dve.wait_ge(s_reduced[b], NS)
                dve.tensor_reduce(neg_max[:], tile_max[:, b], AX.X, ALU.max, negate=True).then_inc(max_ready[b], 1)

            def normalise(h, b):
                sums = turned.rearrange("p b (k r) -> p b k r", r=HW)
                out_heads = heads[:].rearrange("p b (h d) -> p b h d", d=D)[:, :, bass.ds(h - (UNROLL - 1), UNROLL), :]
                dve.wait_ge(ctx_turned[b], 1)
                dve.reciprocal(recip[:], sums[:, :, :, D]).then_inc(recip_ready, 1)
                dve.wait_ge(recip_ready, 1)
                dve.sem_clear(recip_ready)
                dve.tensor_tensor(out_heads, sums[:, :, :, 0:D],
                                  recip[:].rearrange("p b (k o) -> p b k o", o=1).broadcast_to([BT, NB, UNROLL, D]),
                                  ALU.mult).then_inc(normalised[b], 1)

            dve.wait_ge(constants, MASK_DONE)
            for u in range(NS):
                reduce_tile(0, u)
            negate_max(0)
            for u in range(EARLY):
                reduce_tile(1, u)

            def step(h, b, more2):
                nxt, old = (b + 1) % UNROLL, (b + 2) % UNROLL
                for u in range(EARLY, NS):
                    reduce_tile(nxt, u)
                negate_max(nxt)
                if more2:
                    for u in range(EARLY):
                        reduce_tile(old, u)
                if b == UNROLL - 1:
                    normalise(h, b)

            with dve.Fori(0, LOOPS) as it:
                for k in range(UNROLL):
                    step(it * UNROLL + k, k, True)
            for h in range(LOOPS * UNROLL, H - 1):
                step(h, h % UNROLL, h + 2 < H)

            count = [0]

            def weight_step(ins):
                ins.then_inc(weights_ready, 1)
                count[0] += 1
                dve.wait_ge(weights_ready, count[0])

            dve.wait_ge(tail_loaded, 64)
            weight_step(dve.tensor_scalar(w_t[:, 0, :], wf_sb[:], 448.0, -448.0, ALU.min, ALU.max))
            weight_step(dve.tensor_scalar(w_t[:, 1, :], wf_sb[:], 240.0, -240.0, ALU.min, ALU.max))
            weight_step(dve.tensor_scalar(w8[:, 0, :], w_t[:, 1, :], 1.0, None, ALU.mult, saturate=False))
            weight_step(dve.tensor_scalar(w8[:, 1, :], w_t[:, 0, :], 0.5, None, ALU.mult, saturate=False))
            weight_step(dve.tensor_tensor(w_t[:, 2, :], w_t[:, 0, :], w_t[:, 0, :], ALU.mult))
            weight_step(dve.tensor_scalar(w_t[:, 2, :], w_t[:, 2, :], 128.0 ** 2, None, ALU.is_ge))
            weight_step(dve.scalar_tensor_tensor(out=w_t[:, 3, :], in0=w8[:, 1, :], scalar=2.0, in1=w8[:, 0, :],
                                                 op0=ALU.mult, op1=ALU.subtract))
            weight_step(dve.tensor_tensor(w_t[:, 1, :], w_t[:, 3, :], w_t[:, 2, :], ALU.mult))
            weight_step(dve.tensor_tensor(w_q[:], w_t[:, 1, :], w8[:, 0, :], ALU.add))
            assert count[0] == WEIGHT_STEPS

            def chunk(tensor, c):
                return tensor[:, c * BC:(c + 1) * BC]

            def flat(tensor, c):
                return chunk(tensor, c).rearrange("p b e -> p (b e)")

            def copy_last_sums(c):
                dve.wait_ge(p_used[LAST], LAST_ENDS[c])
                dve.tensor_copy(ctx_sb[:, c * BT:(c + 1) * BT], chunk_bank[c][:, 0:BT]).then_inc(sums_copied, 1)

            def normalise_last(c):
                sums = chunk_bank[c][:, 0:BC * HW].rearrange("p (b d) -> p b d", d=HW)
                inverse = chunk(recip, c)[:, :, 0:1]
                dve.wait_ge(sums_turned, c + 1)
                dve.reciprocal(inverse, sums[:, :, D:HW]).then_inc(sums_inverted, 1)
                dve.wait_ge(sums_inverted, c + 1)
                dve.tensor_tensor(chunk(heads, c)[:, :, E - D:], sums[:, :, 0:D],
                                  inverse.broadcast_to([BT, BC, D]), ALU.mult).then_inc(heads_ready, 1)

            def copy_heads(c):
                dve.wait_ge(heads_turned, c + 1)
                dve.tensor_copy(heads_t[:, c, :], chunk_bank[c][:]).then_inc(heads_copied, 1)

            def moments(c, which, src, stats_done, done):
                for t in range(c * BC, (c + 1) * BC):
                    dve.bn_stats(stats[:, which, t, :], src[:, t, :]).then_inc(stats_done, 1)
                for t in range(c * BC, (c + 1) * BC):
                    dve.wait_ge(stats_done, t + 1)
                    ins = dve.bn_aggr(mv[:, which, t, :], stats[:, which, t, :])
                ins.then_inc(done, 1)

            def residual(c):
                dve.wait_ge(attn_ready, c + 1)
                dve.tensor_tensor(flat(z, c), chunk_bank[c][:], flat(x_sb, c), ALU.add).then_inc(z_ready, 1)
                dve.wait_ge(z_ready, c + 1)
                moments(c, 0, z, z_stats, z_moments)

            def round_y(c):
                dve.wait_ge(y_ready, c + 1)
                dve.tensor_copy(chunk(y8, c), chunk(y, c), saturate=False).then_inc(y_rounded, 1)

            def second_residual(c):
                dve.wait_ge(y_biased, c + 1)
                dve.wait_ge(ffn_rounded, c + 1)
                dve.tensor_tensor(chunk(y, c), chunk(y, c), chunk(f_h, c), ALU.add).then_inc(r_ready, 1)
                dve.wait_ge(r_ready, c + 1)
                moments(c, 1, y, r_stats, r_moments)

            def scale_shift(c, which, moments_done, dev_ready, inverted, shifted):
                rs = chunk(rstd[:, which], c)
                dve.wait_ge(dev_ready, c + 1)
                dve.reciprocal(rs, chunk(dev[:, which], c)).then_inc(inverted, 1)
                dve.wait_ge(inverted, c + 1)
                dve.wait_ge(moments_done, c + 1)
                dve.scalar_tensor_tensor(out=chunk(shift[:, which], c), in0=chunk(mv[:, which], c)[:, :, 0],
                                         scalar=-1.0, in1=rs, op0=ALU.mult, op1=ALU.mult).then_inc(shifted, 1)

            def last_norm(c):
                dve.wait_ge(r_dev, c + 1)
                dve.reciprocal(chunk(rstd[:, 1], c), chunk(dev[:, 1], c)).then_inc(r_inverted, 1)
                dve.wait_ge(r_inverted, c + 1)
                dve.wait_ge(r_moments, c + 1)
                for t in range(c * BC, (c + 1) * BC):
                    ins = dve.tensor_scalar(z[:, t, :], y[:, t, :], mv[:, 1, t, 0:1], rstd[:, 1, t:t + 1],
                                            ALU.subtract, ALU.mult)
                ins.then_inc(last_out_ready, 1)

            def first_scale(c):
                scale_shift(c, 0, z_moments, z_dev, z_inverted, z_shift)

            def second_scale(c):
                scale_shift(c, 1, r_moments, r_dev, r_inverted, r_shift)

            normalise_last(0)
            copy_heads(0)
            normalise_last(1)
            residual(0)
            copy_heads(1)
            residual(1)
            normalise_last(2)
            copy_heads(2)
            copy_last_sums(3)
            first_scale(0)
            first_scale(1)
            normalise_last(3)
            residual(2)
            round_y(0)
            round_y(1)
            first_scale(2)
            residual(3)
            round_y(2)
            first_scale(3)
            second_residual(0)
            round_y(3)
            second_residual(1)
            second_scale(0)
            second_residual(2)
            second_scale(1)
            second_residual(3)
            second_scale(2)
            last_norm(3)


_INS = ["x", "xT", "wqT", "wk_down", "wv_down", "q2lT", "v_upT", "woutT", "ffn_wT", "ffn_bias"]


def kernel(L0_attn_hidden_states, L0_attn_Wq, L0_attn_Wk_down, L0_attn_Wv_down, L0_attn_q_to_latent,
           L0_attn_v_up, L0_attn_Wout, L0_ffn_weight, L0_ffn_bias):
    import numpy as np
    import concourse.bacc as bacc
    from concourse import mybir as _mybir
    from concourse.bass_utils import run_bass_kernel_spmd

    x = np.asarray(L0_attn_hidden_states)[0]
    T, E = x.shape
    H, D, L = L0_attn_q_to_latent.shape
    laid = {
        "x": x,
        "xT": x.T,
        "wqT": np.asarray(L0_attn_Wq).T,
        "wk_down": np.asarray(L0_attn_Wk_down),
        "wv_down": np.asarray(L0_attn_Wv_down),
        "q2lT": np.asarray(L0_attn_q_to_latent).reshape(H * D, L).T,
        "v_upT": np.asarray(L0_attn_v_up).transpose(1, 0, 2).reshape(L, H * D),
        "woutT": np.asarray(L0_attn_Wout).T,
        "ffn_wT": np.asarray(L0_ffn_weight).T,
        "ffn_bias": np.asarray(L0_ffn_bias),
    }
    nc = bacc.Bacc("TRN2", target_bir_lowering=False, num_devices=1)
    arrays, args = {}, []
    for name in _INS:
        a = np.ascontiguousarray(laid[name])
        arrays[f"in_{name}"] = a
        args.append(nc.dram_tensor(f"in_{name}", a.shape, _mybir.dt.from_np(a.dtype), kind="ExternalInput").ap())
    out = nc.dram_tensor("out", (T, E), _mybir.dt.from_np(x.dtype), kind="ExternalOutput").ap()
    postln_block_kernel(nc, *args, out)
    r = run_bass_kernel_spmd(nc, [arrays], core_ids=[0])
    return r.results[0]["out"].reshape(1, T, E)
```
